# Optimizing a Trainium2 kernel written in Bass

```python
import numpy as np
import jax
import jax.numpy as jnp

def _softmax(x, axis=-1):
    return jax.nn.softmax(x, axis=axis)

def _gelu(x):
    return jax.nn.gelu(x, approximate=True)

def _silu(x):
    return jax.nn.silu(x)

def _sigmoid(x):
    return jax.nn.sigmoid(x)

def _layernorm(x, axis=-1, eps=1e-05):
    m = jnp.mean(x, axis=axis, keepdims=True)
    v = jnp.var(x, axis=axis, keepdims=True)
    return (x - m) / jnp.sqrt(v + eps)

def _scatter_add(tgt, idx, src, axis=0):
    return tgt.at[idx].add(src)

def _segment_sum(src, seg, n):
    return jax.ops.segment_sum(src, seg, n)
kernel_name = 'mk_gnn_resnorm_d1_gnn_r8_b1df4f'

def setup_inputs(seed: int=0):
    np.random.seed(seed)
    _w = jnp.asarray

    def _rec_inputs():
        import jax
        import jax.numpy as jnp
        _gk = jax.random.key(seed)
        x = -0.0005121 + 1.001 * jax.random.normal(jax.random.fold_in(_gk, 1), (6250, 64), jnp.float32)
        src = jax.random.randint(jax.random.fold_in(_gk, 2), (200000,), 0, 6250, jnp.int32)
        dst = jnp.minimum((6250 * jax.random.uniform(jax.random.fold_in(_gk, 3), (200000,)) ** 2.0).astype(jnp.int32), 49999)
        _o = jnp.argsort(dst, stable=True)
        src = src[_o]
        dst = dst[_o]
        edge_attr_64 = -6.74381e-05 + 0.999835 * jax.random.normal(jax.random.fold_in(_gk, 11), (200000, 64), jnp.float32)
        return (x, src, dst, edge_attr_64)
    x, src, dst, edge_attr_64 = _rec_inputs()

    def _L0_gnn_setup():
        import jax, jax.numpy as jnp
        import numpy as np
        N_NODES = 6250
        N_EDGES = 156250
        D_NODE = 64
        D_EDGE = 64
        M_OUT = 64
        U_OUT = 64
        key = jax.random.key(seed)
        k1, k2, k3, k4, k5, k6 = jax.random.split(key, 6)
        H = jax.random.normal(k1, (N_NODES, D_NODE), dtype=jnp.float32)
        Xe = jax.random.normal(k2, (N_EDGES, D_EDGE), dtype=jnp.float32)
        id_Xe = jax.random.randint(k3, (2, N_EDGES), 0, N_NODES, dtype=jnp.int64)
        M_W = jax.random.normal(k4, (M_OUT, D_NODE + D_EDGE), dtype=jnp.float32) * 0.05
        M_b = jnp.zeros((M_OUT,), dtype=jnp.float32)
        U_W = jax.random.normal(k5, (U_OUT, D_NODE + M_OUT), dtype=jnp.float32) * 0.05
        U_b = jnp.zeros((U_OUT,), dtype=jnp.float32)
        return {'H': H, 'Xe': Xe, 'id_Xe': id_Xe, 'M_W': M_W, 'M_b': M_b, 'U_W': U_W, 'U_b': U_b}
    _L0_gnn_all = _L0_gnn_setup()
    _L0_gnn_in = {k: v for k, v in _L0_gnn_all.items() if k in ('M_W', 'M_b', 'U_W', 'U_b')}
    del _L0_gnn_all
    return {'x': x, 'src': src, 'dst': dst, 'edge_attr_64': edge_attr_64, 'L0_gnn_M_W': _L0_gnn_in['M_W'], 'L0_gnn_M_b': _L0_gnn_in['M_b'], 'L0_gnn_U_W': _L0_gnn_in['U_W'], 'L0_gnn_U_b': _L0_gnn_in['U_b']}

def reference(x, src, dst, edge_attr_64, L0_gnn_M_W, L0_gnn_M_b, L0_gnn_U_W, L0_gnn_U_b):
    import jax
    import jax.numpy as jnp

    def _L0_gnn_ref(H, Xe, id_Xe, M_W, M_b, U_W, U_b):
        import jax, jax.numpy as jnp
        import numpy as np
        N_NODES = 6250
        N_EDGES = 156250
        D_NODE = 64
        D_EDGE = 64
        M_OUT = 64
        U_OUT = 64
        features = H[id_Xe[0]]
        M_in = jnp.concatenate([features, Xe], axis=1)
        Y = jax.nn.relu(M_in @ M_W.T + M_b)
        Z = jax.ops.segment_sum(Y, id_Xe[1], num_segments=H.shape[0])
        U_in = jnp.concatenate([H, Z], axis=1)
        H_next = jax.nn.relu(U_in @ U_W.T + U_b)
        return H_next
    edge_index = jnp.stack([src, dst])
    x = _layernorm(x + _L0_gnn_ref(x, edge_attr_64, edge_index, L0_gnn_M_W, L0_gnn_M_b, L0_gnn_U_W, L0_gnn_U_b), axis=-1)
    return x

_drawn_inputs = setup_inputs


def setup_inputs(seed=0):
    import zlib

    import numpy as np

    out = dict(_drawn_inputs(seed))
    spreads = {'L0_gnn_M_b': (0.0, 0.1), 'L0_gnn_U_b': (0.0, 0.1)}
    factors = {}
    for name, (base, spread) in spreads.items():
        noise = np.random.default_rng([zlib.crc32(name.encode()), seed]).standard_normal(out[name].shape)
        drawn = base * np.exp(spread * noise) if base else spread * noise
        out[name] = jnp.asarray(drawn.astype(out[name].dtype))
    for name, factor in factors.items():
        out[name] = (out[name] * factor).astype(out[name].dtype)
    return out
```

```python
import numpy as np
import concourse.bass as bass
from concourse import mybir
from contextlib import ExitStack


def gnn_residual_layernorm_kernel(
    nc: bass.Bass,
    x: bass.AP,
    src: bass.AP,
    dst: bass.AP,
    edge_attr: bass.AP,
    M_W: bass.AP,
    M_b: bass.AP,
    U_W: bass.AP,
    U_b: bass.AP,
    out: bass.AP,
):
    fp32 = mybir.dt.float32
    i32 = mybir.dt.int32
    ALU = mybir.AluOpType
    ACT = mybir.ActivationFunctionType
    AX = mybir.AxisListType

    P = 128
    N, D = x.shape
    NE = src.shape[0]
    TILES = 8
    PAIRS = TILES // 2
    CHUNK = TILES * P
    NC = NE // CHUNK
    TAIL = NE - NC * CHUNK
    TP = 64
    TT = TAIL // TP
    SLOTS = 3
    ROUNDS = NC // SLOTS
    W = 128
    NW = -(-N // W)
    NFULL = N // W
    NLAST = N - NFULL * W
    FB = 8
    XB = 4
    EPS = 1e-5
    assert NC % SLOTS == 0 and TAIL == TP * TT and TT <= TILES and P < NC + 1 <= 2 * P
    NB = NC + 1 - P

    edge_chunks = edge_attr[0:NC * CHUNK, :].rearrange("(c p j) d -> c p (j d)", p=P, j=TILES)
    src_chunks = src[0:NC * CHUNK].rearrange("(c p j) -> c p j", p=P, j=TILES)
    dst_chunks = dst[0:NC * CHUNK].rearrange("(c p j) -> c p j", p=P, j=TILES)
    edge_tail = edge_attr[NC * CHUNK:NE, :].rearrange("(p j) d -> p (j d)", p=TP)
    src_tail = src[NC * CHUNK:NE].rearrange("(p j) -> p j", p=TP)
    dst_tail = dst[NC * CHUNK:NE].rearrange("(p j) -> p j", p=TP)
    dst_rows = dst[0:NC * CHUNK].rearrange("(c n) -> c n", n=CHUNK)
    dst_tail_row = dst[NC * CHUNK:NE].rearrange("(c n) -> c n", c=1)
    x_blocks = x[0:NFULL * W, :].rearrange("(b p) d -> p b d", p=W)
    out_blocks = out[0:NFULL * W, :].rearrange("(b p) d -> p b d", p=W)

    ctx = ExitStack()
    with ctx:
        def sb(name, shape, dt=fp32):
            return ctx.enter_context(nc.sbuf_tensor(name, shape, dt))

        def pb(name):
            return ctx.enter_context(nc.psum_tensor(name, [P, 512], fp32))

        def sem(name):
            return ctx.enter_context(nc.semaphore(name))

        def sems(name):
            return [sem(f"{name}{u}") for u in range(SLOTS)]

        srcs = [sb(f"srcs{u}", [P, TILES], i32) for u in range(SLOTS)]
        dsts = [sb(f"dsts{u}", [P, TILES], i32) for u in range(SLOTS)]
        gathered = [sb(f"gathered{u}", [P, TILES * D]) for u in range(SLOTS)]
        edges = [sb(f"edges{u}", [P, TILES * D]) for u in range(SLOTS)]
        gathered_T = [sb(f"gathered_T{u}", [P, PAIRS * P]) for u in range(SLOTS)]
        edges_T = [sb(f"edges_T{u}", [P, PAIRS * P]) for u in range(SLOTS)]
        messages = [sb(f"messages{u}", [P, TILES * D]) for u in range(SLOTS)]
        onehot = [sb(f"onehot{u}", [P, TILES, W]) for u in range(SLOTS)]

        ZX = sb("ZX", [P, NW * W + W])
        xx = sb("xx", [P, NW, 2 * D])
        ident = sb("ident", [P, P])
        count = sb("count", [P, W], i32)
        window_start = sb("window_start", [P, NW])
        window_start_i = sb("window_start_i", [P, NW], i32)
        ones = sb("ones", [1, P])
        w_stage = sb("w_stage", [D, 3, 2 * D])
        w_gathered = sb("w_gathered", [P, 2 * D])
        w_edges = sb("w_edges", [P, 2 * D])
        w_update = sb("w_update", [P, D])
        m_bias = sb("m_bias", [1, TILES, D])
        u_bias = sb("u_bias", [1, FB, D])
        dst_check = sb("dst_check", [P, 2, CHUNK], i32)
        least = sb("least", [P, 2])
        most = sb("most", [P, 2])
        span = sb("span", [P, 2])
        base_row = sb("base_row", [1, 2 * P])
        base_i = sb("base_i", [1, 2 * P], i32)
        base = sb("base", [P, 2 * P])
        widest = sb("widest", [1, 1])
        spread = sb("spread", [1, 1], i32)
        h = sb("h", [P, NW, D])
        sq = sb("sq", [P, NW, D])
        total = sb("total", [P, NW])
        var = sb("var", [P, NW])
        std = sb("std", [P, NW])
        eps_col = sb("eps_col", [P, 1])

        p_edges_T = pb("p_edges_T")
        p_gathered_T = pb("p_gathered_T")
        p_messages = [pb(f"p_messages{u}") for u in range(SLOTS)]
        p_windows = pb("p_windows")
        p_count = pb("p_count")
        p_setup = pb("p_setup")

        s_ident = sem("s_ident")
        s_iota = sem("s_iota")
        s_cleared = sem("s_cleared")
        s_w_loaded = sem("s_w_loaded")
        s_bias_loaded = sem("s_bias_loaded")
        s_x_loaded = sem("s_x_loaded")
        s_check_loaded = sem("s_check_loaded")
        s_check_pad = sem("s_check_pad")
        s_w_T = sem("s_w_T")
        s_w_ready = sem("s_w_ready")
        s_x_T = sem("s_x_T")
        s_x_copied = sem("s_x_copied")
        s_least = sem("s_least")
        s_least_T = sem("s_least_T")
        s_base_row = sem("s_base_row")
        s_base_spread = sem("s_base_spread")
        s_base = sem("s_base")
        s_dve = sem("s_dve")
        s_src_loaded = sems("s_src_loaded")
        s_dst_loaded = sems("s_dst_loaded")
        s_edges_loaded = sems("s_edges_loaded")
        s_gathered = sems("s_gathered")
        s_edges_T = sem("s_edges_T")
        s_edges_T_copied = sem("s_edges_T_copied")
        s_slot_taken = sem("s_slot_taken")
        s_gathered_T = sem("s_gathered_T")
        s_gathered_T_copied = sem("s_gathered_T_copied")
        s_summed = sem("s_summed")
        s_messages = sem("s_messages")
        s_onehot = sem("s_onehot")
        s_chunk_added = sem("s_chunk_added")
        s_window = sem("s_window")
        s_window_added = sem("s_window_added")
        s_update = sem("s_update")
        s_h = sem("s_h")
        s_centered = sem("s_centered")
        s_squared = sem("s_squared")
        s_var = sem("s_var")
        s_std = sem("s_std")
        s_scale = sem("s_scale")
        s_normed = sem("s_normed")
        s_out = sem("s_out")

        groups = [(b, min(b + FB, NW)) for b in range(0, NW, FB)]
        x_groups = [(b, min(b + XB, NW)) for b in range(0, NW, XB)]

        block = ctx.enter_context(nc.Block())

        @block.sync
        def _(sp):
            def load_src(chunk, u):
                sp.dma_start(srcs[u][:, :], src_chunks[chunk]).then_inc(s_src_loaded[u], 16)

            def load_dst(chunk, u):
                sp.dma_start(dsts[u][:, :], dst_chunks[chunk]).then_inc(s_dst_loaded[u], 16)

            def load_edges(chunk, u):
                sp.dma_start(edges[u][:, :], edge_chunks[chunk]).then_inc(s_edges_loaded[u], 16)

            for u in range(SLOTS):
                load_src(u, u)
            for k, w in enumerate((M_W[:, 0:D], M_W[:, 0:D], M_W[:, D:2 * D], M_W[:, D:2 * D],
                                   U_W[:, D:2 * D], U_W[:, 0:D])):
                sp.dma_start(w_stage[:, k // 2, (k % 2) * D:(k % 2 + 1) * D], w).then_inc(s_w_loaded, 16)
            sp.dma_start(m_bias[:, :, :], M_b.rearrange("(a b d) -> a b d", a=1, b=1)
                         .to_broadcast([1, TILES, D])).then_inc(s_bias_loaded, 16)
            sp.dma_start(u_bias[:, :, :], U_b.rearrange("(a b d) -> a b d", a=1, b=1)
                         .to_broadcast([1, FB, D])).then_inc(s_bias_loaded, 16)
            for u in range(SLOTS):
                load_edges(u, u)
                load_dst(u, u)
            with sp.Fori(1, ROUNDS) as r:
                for u in range(SLOTS):
                    chunk = r * SLOTS + u
                    sp.wait_ge(s_edges_T, chunk - (SLOTS - 1))
                    load_edges(chunk, u)
                    sp.wait_ge(s_chunk_added, chunk - (SLOTS - 1))
                    load_dst(chunk, u)
                    sp.wait_ge(s_gathered[u], r * (16 * TILES))
                    load_src(chunk, u)
            sp.wait_ge(s_edges_T, NC - (SLOTS - 1))
            sp.dma_start(edges[0][0:TP, 0:TT * D], edge_tail).then_inc(s_edges_loaded[0], 16)
            sp.wait_ge(s_gathered[0], ROUNDS * 16 * TILES)
            sp.dma_start(srcs[0][0:TP, 0:TT], src_tail).then_inc(s_src_loaded[0], 16)
            sp.wait_ge(s_cleared, 2)
            sp.dma_start(dsts[0][0:TP, 0:TT], dst_tail).then_inc(s_dst_loaded[0], 16)

            for g, (b0, b1) in enumerate(groups):
                sp.wait_ge(s_normed, g + 1)
                full = min(b1, NFULL)
                if full > b0:
                    sp.dma_start(out_blocks[:, b0:full, :], h[:, b0:full, :]).then_inc(s_out, 16)
                if b1 > NFULL:
                    sp.dma_start(out[NFULL * W:N, :], h[0:NLAST, NFULL, :]).then_inc(s_out, 16)
            stores = sum((min(b1, NFULL) > b0) + (b1 > NFULL) for b0, b1 in groups)
            sp.wait_ge(s_out, 16 * stores)

        @block.gpsimd
        def _(pool):
            nc.gpsimd.memset(ident[:, :], 0.0).then_inc(s_ident, 1)
            pool.wait_ge(s_ident, 1)
            nc.gpsimd.affine_select(out=ident[:, :], in_=ident[:, :], compare_op=ALU.not_equal, fill=1.0,
                                    base=0, pattern=[[-1, P]], channel_multiplier=1).then_inc(s_ident, 1)
            nc.gpsimd.iota(count[:, :], pattern=[[1, W]], base=0, channel_multiplier=0)
            nc.gpsimd.iota(window_start_i[:, :], pattern=[[W, NW]], base=0,
                           channel_multiplier=0).then_inc(s_iota, 1)

            def gather(u, parts=P, tiles=TILES):
                for j in range(tiles):
                    nc.gpsimd.indirect_dma_start(
                        out=gathered[u][0:parts, j * D:(j + 1) * D], out_offset=None, in_=x[:, :],
                        in_offset=bass.IndirectOffsetOnAxis(ap=srcs[u][0:parts, j:j + 1], axis=0),
                    ).then_inc(s_gathered[u], 16)

            for u in range(SLOTS):
                pool.wait_ge(s_src_loaded[u], 16)
                gather(u)
            with pool.Fori(1, ROUNDS) as r:
                for u in range(SLOTS):
                    pool.wait_ge(s_src_loaded[u], (r + 1) * 16)
                    pool.wait_ge(s_gathered_T, r * SLOTS + (u - SLOTS + 1))
                    pool.sem_inc(s_slot_taken, 1)
                    gather(u)
            pool.wait_ge(s_src_loaded[0], (ROUNDS + 1) * 16)
            pool.wait_ge(s_gathered_T, NC - SLOTS + 1)
            gather(0, TP, TT)

            for g, (b0, b1) in enumerate(groups):
                pool.wait_ge(s_scale, g + 1)
                nc.gpsimd.tensor_tensor(h[:, b0:b1, :], h[:, b0:b1, :],
                                        std[:, b0:b1].unsqueeze(2).to_broadcast([P, b1 - b0, D]),
                                        ALU.mult).then_inc(s_normed, 1)

        @block.scalar
        def _(act):
            act.dma_start(dst_check[:, 0, :], dst_rows[0:P, :]).then_inc(s_check_loaded, 16)
            act.dma_start(dst_check[0:NB - 1, 1, :], dst_rows[P:NC, :]).then_inc(s_check_loaded, 16)
            for c in range(0, CHUNK, TAIL):
                n = min(TAIL, CHUNK - c)
                act.dma_start(dst_check[NB - 1:NB, 1, c:c + n], dst_tail_row[:, 0:n]).then_inc(s_check_loaded, 16)
            act.wait_ge(s_cleared, 1)
            for k in range(2):
                act.dma_start(xx[:, 0:NFULL, k * D:(k + 1) * D], x_blocks).then_inc(s_x_loaded, 16)
                act.dma_start(xx[0:NLAST, NFULL, k * D:(k + 1) * D], x[NFULL * W:N, :]).then_inc(s_x_loaded, 16)

            for g, (b0, b1) in enumerate(x_groups):
                act.wait_ge(s_x_T, g + 1)
                nc.scalar.copy(ZX[D:P, b0 * W:b1 * W],
                               p_messages[g % SLOTS][D:P, 0:(b1 - b0) * W]).then_inc(s_x_copied, 1)

            def copy_edges_T(chunk, u):
                act.wait_ge(s_edges_T, chunk + 1)
                nc.scalar.copy(edges_T[u][:, :], p_edges_T[:, :]).then_inc(s_edges_T_copied, 1)

            def copy_gathered_T(chunk, u):
                act.wait_ge(s_gathered_T, chunk + 1)
                nc.scalar.copy(gathered_T[u][:, :], p_gathered_T[:, :]).then_inc(s_gathered_T_copied, 1)

            def rectify(chunk, u):
                act.wait_ge(s_summed, chunk + 1)
                nc.scalar.activation(messages[u][:, :], p_messages[u][:, :], ACT.Relu).then_inc(s_messages, 1)

            copy_edges_T(0, 0)
            with act.Fori(0, ROUNDS) as r:
                for u in range(SLOTS):
                    chunk = r * SLOTS + u
                    copy_gathered_T(chunk, u)
                    copy_edges_T(chunk + 1, (u + 1) % SLOTS)
                    rectify(chunk, u)
            copy_gathered_T(NC, 0)
            rectify(NC, 0)

            def relu_update(g):
                b0, b1 = groups[g]
                act.wait_ge(s_update, g + 1)
                nc.scalar.activation(sq[:, b0:b1, :],
                                     p_messages[g % SLOTS][:, 0:(b1 - b0) * D].rearrange("p (b d) -> p b d", d=D),
                                     ACT.Relu).then_inc(s_h, 1)

            def square(g):
                b0, b1 = groups[g]
                act.wait_ge(s_centered, g + 1)
                nc.scalar.activation(sq[:, b0:b1, :], h[:, b0:b1, :], ACT.Square).then_inc(s_squared, 1)

            def root(g):
                b0, b1 = groups[g]
                act.wait_ge(s_var, g + 1)
                nc.scalar.activation(std[:, b0:b1], var[:, b0:b1], ACT.Sqrt, bias=eps_col[:, 0:1],
                                     scale=1.0 / D).then_inc(s_std, 1)

            for g in range(len(groups) + 2):
                if g < len(groups):
                    relu_update(g)
                if 1 <= g <= len(groups):
                    square(g - 1)
                if g >= 2:
                    root(g - 2)

        @block.vector
        def _(dve):
            chain = [0]

            def link(ins):
                chain[0] += 1
                ins.then_inc(s_dve, 1)
                dve.wait_ge(s_dve, chain[0])

            nc.vector.memset(xx[:, NFULL, :], 0.0).then_inc(s_cleared, 1)
            nc.vector.memset(ones[:, :], 1.0)
            nc.vector.memset(eps_col[:, :], EPS)
            nc.vector.memset(w_gathered[:, :], 0.0)
            nc.vector.memset(w_edges[:, :], 0.0)
            link(nc.vector.memset(ZX[0:D, :], 0.0))
            dve.wait_ge(s_iota, 1)
            nc.vector.tensor_copy(p_count[:, 0:W], count[:, :])
            link(nc.vector.tensor_copy(window_start[:, :], window_start_i[:, :]))
            dve.wait_ge(s_w_T, 1)
            nc.vector.tensor_copy(w_gathered[0:D, 0:D], p_setup[0:D, 0:D])
            nc.vector.tensor_copy(w_gathered[D:P, D:2 * D], p_setup[D:P, 0:D])
            nc.vector.tensor_copy(w_edges[0:D, 0:D], p_setup[0:D, D:2 * D])
            nc.vector.tensor_copy(w_edges[D:P, D:2 * D], p_setup[D:P, D:2 * D])
            nc.vector.tensor_copy(w_update[:, :], p_setup[:, 2 * D:3 * D]).then_inc(s_w_ready, 1)
            dve.wait_ge(s_check_loaded, 16 * (2 + -(-CHUNK // TAIL)))
            for k, n in ((0, P), (1, NB)):
                nc.vector.tensor_reduce(least[0:n, k:k + 1], dst_check[0:n, k, :], AX.X, ALU.min)
                link(nc.vector.tensor_reduce(most[0:n, k:k + 1], dst_check[0:n, k, :], AX.X, ALU.max))
                last = nc.vector.tensor_tensor(span[0:n, k:k + 1], most[0:n, k:k + 1], least[0:n, k:k + 1],
                                               ALU.subtract)
            last.then_inc(s_least, 1)
            dve.wait_ge(s_least_T, 1)
            nc.vector.tensor_copy(base_row[:, 0:NC + 1], p_setup[0:1, 0:NC + 1]).then_inc(s_base_row, 1)
            nc.vector.tensor_copy(base_i[:, 0:NC + 1], p_setup[0:1, 0:NC + 1])
            link(nc.vector.reduce_max(widest[:, :], p_setup[0:1, 256:256 + NC + 1], AX.X))
            nc.vector.tensor_scalar(spread[:, :], widest[:, :], float(W), None, ALU.is_ge).then_inc(s_base, 1)
            dve.wait_ge(s_base_spread, 1)
            link(nc.vector.tensor_copy(base[:, 0:NC + 1], p_windows[:, 0:NC + 1]))
            dve.wait_ge(s_base, 1)

            count_b = p_count[:, 0:W].unsqueeze(1).to_broadcast([P, TILES, W])

            def compare(u, start):
                nc.vector.scalar_tensor_tensor(
                    out=onehot[u][:, :, :], in0=count_b, scalar=start,
                    in1=dsts[u][:, :].unsqueeze(2).to_broadcast([P, TILES, W]),
                    op0=ALU.add, op1=ALU.is_equal).then_inc(s_onehot, 1)

            def clear_tail_dst():
                nc.vector.memset(dsts[0][:, :], -1).then_inc(s_cleared, 1)

            def one_window(chunk, u, dst_count):
                dve.wait_ge(s_dst_loaded[u], dst_count)
                compare(u, base[:, bass.ds(chunk, 1)])
                start = dve.value_load(base_i[0:1, bass.ds(chunk, 1)], min_val=0, max_val=N - 1)
                dve.wait_ge(s_window, chunk + 1)
                columns = ZX[0:D, bass.ds(start, W)]
                nc.vector.tensor_tensor(columns, columns, p_windows[0:D, u * W:(u + 1) * W],
                                        ALU.add).then_inc(s_chunk_added, 1)

            def all_windows(chunk, u, dst_count):
                with dve.Fori(0, NW) as w:
                    dve.wait_ge(s_dst_loaded[u], dst_count)
                    compare(u, window_start[:, bass.ds(w, 1)])
                    dve.wait_ge(s_window, chunk * NW + w + 1)
                    columns = ZX[0:D, bass.ds(w * W, W)]
                    nc.vector.tensor_tensor(columns, columns, p_windows[0:D, u * W:(u + 1) * W],
                                            ALU.add).then_inc(s_window_added, 1)
                dve.wait_ge(s_window_added, (chunk + 1) * NW)
                dve.sem_inc(s_chunk_added, 1)

            def chunks(windows):
                with dve.Fori(0, ROUNDS) as r:
                    for u in range(SLOTS):
                        windows(r * SLOTS + u, u, (r + 1) * 16)
                clear_tail_dst()
                windows(NC, 0, (ROUNDS + 1) * 16)

            is_spread = dve.value_load(spread[0:1, 0:1], min_val=0, max_val=1)
            with dve.If(is_spread == 0):
                chunks(one_window)
            with dve.Else():
                chunks(all_windows)

            def center(g):
                b0, b1 = groups[g]
                n = b1 - b0
                hg = h[:, b0:b1, :]
                dve.wait_ge(s_h, g + 1)
                link(nc.vector.tensor_tensor(hg, sq[:, b0:b1, :], xx[:, b0:b1, 0:D], ALU.add))
                link(nc.vector.reduce_sum(total[:, b0:b1], hg, AX.X))
                nc.vector.scalar_tensor_tensor(out=hg, in0=total[:, b0:b1].unsqueeze(2).to_broadcast([P, n, D]),
                                               scalar=-1.0 / D, in1=hg, op0=ALU.mult,
                                               op1=ALU.add).then_inc(s_centered, 1)

            def sum_squares(g):
                b0, b1 = groups[g]
                dve.wait_ge(s_squared, g + 1)
                nc.vector.reduce_sum(var[:, b0:b1], sq[:, b0:b1, :], AX.X).then_inc(s_var, 1)

            def invert(g):
                b0, b1 = groups[g]
                dve.wait_ge(s_std, g + 1)
                nc.vector.reciprocal(std[:, b0:b1], std[:, b0:b1]).then_inc(s_scale, 1)

            for g in range(len(groups) + 2):
                if g < len(groups):
                    center(g)
                if 1 <= g <= len(groups):
                    sum_squares(g - 1)
                if g >= 2:
                    invert(g - 2)

        @block.tensor
        def _(pe):
            pe.wait_ge(s_ident, 2)
            pe.wait_ge(s_w_loaded, 6 * 16)
            for k in range(3):
                last = nc.tensor.transpose(p_setup[:, k * D:(k + 1) * D], w_stage[:, k, :], ident[0:D, 0:D])
            last.then_inc(s_w_T, 1)
            pe.wait_ge(s_x_loaded, 4 * 16)
            for g, (b0, b1) in enumerate(x_groups):
                if g >= SLOTS:
                    pe.wait_ge(s_x_copied, g - SLOTS + 1)
                for b in range(b0, b1):
                    last = nc.tensor.transpose(p_messages[g % SLOTS][:, (b - b0) * W:(b - b0 + 1) * W],
                                               xx[:, b, :], ident[:, :])
                last.then_inc(s_x_T, 1)
            pe.wait_ge(s_least, 1)
            for k, n in ((0, P), (1, NB)):
                nc.tensor.transpose(p_setup[0:1, k * P:k * P + n], least[0:n, k:k + 1], ident[0:n, 0:n])
                last = nc.tensor.transpose(p_setup[0:1, 256 + k * P:256 + k * P + n], span[0:n, k:k + 1],
                                           ident[0:n, 0:n])
            last.then_inc(s_least_T, 1)
            pe.wait_ge(s_base_row, 1)
            nc.tensor.matmul(p_windows[:, 0:NC + 1], ones[0:1, :], base_row[0:1, 0:NC + 1],
                             start=True, stop=True).then_inc(s_base_spread, 1)
            pe.wait_ge(s_x_copied, len(x_groups))
            pe.wait_ge(s_bias_loaded, 2 * 16)

            def transpose_edges(u, edges_count):
                pe.wait_ge(s_edges_loaded[u], edges_count)
                for q in range(PAIRS):
                    last = nc.tensor.transpose(p_edges_T[:, q * P:(q + 1) * P], edges[u][:, q * P:(q + 1) * P],
                                               ident[:, :])
                last.then_inc(s_edges_T, 1)

            def add_edges(chunk, u):
                nc.tensor.matmul(p_messages[u][:, :], ones[0:1, :], m_bias[0:1, :, :].rearrange("a b d -> a (b d)"),
                                 start=True, stop=False)
                pe.wait_ge(s_edges_T_copied, chunk + 1)
                for q in range(PAIRS):
                    nc.tensor.matmul(p_messages[u][:, q * P:(q + 1) * P], edges_T[u][:, q * P:(q + 1) * P],
                                     w_edges[:, :], start=False, stop=False)

            def transpose_gathered(u, gathered_count):
                pe.wait_ge(s_gathered[u], gathered_count)
                for q in range(PAIRS):
                    last = nc.tensor.transpose(p_gathered_T[:, q * P:(q + 1) * P],
                                               gathered[u][:, q * P:(q + 1) * P], ident[:, :])
                last.then_inc(s_gathered_T, 1)

            def add_gathered(chunk, u):
                pe.wait_ge(s_gathered_T_copied, chunk + 1)
                for q in range(PAIRS):
                    last = nc.tensor.matmul(p_messages[u][:, q * P:(q + 1) * P],
                                            gathered_T[u][:, q * P:(q + 1) * P], w_gathered[:, :],
                                            start=False, stop=(q == PAIRS - 1))
                last.then_inc(s_summed, 1)

            def sum_window(u):
                for j in range(TILES):
                    last = nc.tensor.matmul(p_windows[0:D, u * W:(u + 1) * W], messages[u][:, j * D:(j + 1) * D],
                                            onehot[u][:, j, :], start=(j == 0), stop=(j == TILES - 1))
                last.then_inc(s_window, 1)

            def one_window(chunk, u):
                pe.wait_ge(s_messages, chunk + 1)
                pe.wait_ge(s_onehot, chunk + 1)
                sum_window(u)

            def all_windows(chunk, u):
                with pe.Fori(0, NW) as w:
                    pe.wait_ge(s_messages, chunk + 1)
                    pe.wait_ge(s_onehot, chunk * NW + w + 1)
                    sum_window(u)

            def chunks(windows):
                transpose_edges(0, 16)
                add_edges(0, 0)
                with pe.Fori(0, ROUNDS) as r:
                    for u in range(SLOTS):
                        chunk, v = r * SLOTS + u, (u + 1) % SLOTS
                        transpose_gathered(u, (r + 1) * (16 * TILES))
                        transpose_edges(v, (r + (2 if u == SLOTS - 1 else 1)) * 16)
                        add_gathered(chunk, u)
                        add_edges(chunk + 1, v)
                        windows(chunk, u)
                transpose_gathered(0, (ROUNDS * TILES + TT) * 16)
                add_gathered(NC, 0)
                windows(NC, 0)

            pe.wait_ge(s_base, 1)
            is_spread = pe.value_load(spread[0:1, 0:1], min_val=0, max_val=1)
            with pe.If(is_spread == 0):
                chunks(one_window)
            with pe.Else():
                chunks(all_windows)

            pe.wait_ge(s_chunk_added, NC + 1)
            for g, (b0, b1) in enumerate(groups):
                if g >= SLOTS:
                    pe.wait_ge(s_h, g - SLOTS + 1)
                n = (b1 - b0) * D
                nc.tensor.matmul(p_messages[g % SLOTS][:, 0:n], ones[0:1, :],
                                 u_bias[0:1, 0:b1 - b0, :].rearrange("a b d -> a (b d)"), start=True, stop=False)
                for b in range(b0, b1):
                    last = nc.tensor.matmul(p_messages[g % SLOTS][:, (b - b0) * D:(b - b0 + 1) * D],
                                            ZX[:, b * W:(b + 1) * W], w_update[:, :],
                                            start=False, stop=(b == b1 - 1))
                last.then_inc(s_update, 1)


_INS = ['x', 'src', 'dst', 'edge_attr_64', 'L0_gnn_M_W', 'L0_gnn_M_b', 'L0_gnn_U_W', 'L0_gnn_U_b']
_OUTS = [((6250, 64), 'float32')]


def kernel(**inputs):
    import numpy as _np
    import concourse.bacc as _bacc
    from concourse import mybir as _mybir
    from concourse.bass_utils import run_bass_kernel_spmd as _run

    nc = _bacc.Bacc("TRN2", target_bir_lowering=False, num_devices=1)
    arrays, args = {}, []
    for name in _INS:
        a = _np.ascontiguousarray(inputs[name])
        arrays[f"in_{name}_dram"] = a
        args.append(nc.dram_tensor(f"in_{name}_dram", a.shape, _mybir.dt.from_np(a.dtype), kind="ExternalInput").ap())
    for i, (shape, dtype) in enumerate(_OUTS):
        dt = _mybir.dt.from_np(_np.dtype(dtype))
        args.append(nc.dram_tensor(f"out_{i}_dram", shape, dt, kind="ExternalOutput").ap())
    gnn_residual_layernorm_kernel(nc, *args)
    r = _run(nc, [arrays], core_ids=[0])
    return r.results[0]["out_0_dram"]
```

```python
import numpy as np
import concourse.bass as bass
from concourse import mybir
from contextlib import ExitStack


def gnn_residual_layernorm_kernel(
    nc: bass.Bass,
    x: bass.AP,
    src: bass.AP,
    dst: bass.AP,
    edge_attr: bass.AP,
    M_W: bass.AP,
    M_b: bass.AP,
    U_W: bass.AP,
    U_b: bass.AP,
    out: bass.AP,
):
    fp32 = mybir.dt.float32
    bf16 = mybir.dt.bfloat16
    i32 = mybir.dt.int32
    ALU = mybir.AluOpType
    ACT = mybir.ActivationFunctionType
    AX = mybir.AxisListType

    P = 128
    N, D = x.shape
    NE = src.shape[0]
    TILES = 8
    PAIRS = TILES // 2
    CHUNK = TILES * P
    NC = NE // CHUNK
    TAIL = NE - NC * CHUNK
    TW = TAIL // P
    TP = TAIL - TW * P
    TT = TW + 1
    TQ = -(-TT // 2)
    SLOTS = 3
    PT = TILES - 1
    PE_EDGES = PT * P
    PICKED = (1, 2)
    NP = len(PICKED)
    ROUNDS = NC // SLOTS
    W = 128
    NW = -(-N // W)
    NFULL = N // W
    NLAST = N - NFULL * W
    MISS = 8192.0
    assert N <= MISS and P == 128
    PARTS = [(0, 17), (17, 33), (33, NW)]
    FB = 8
    XB = 4
    X_FIRST = NFULL // 2 // XB * XB
    EPS = 1e-5

    def gathered_by(r, u):
        return r * (16 * (PT if u in PICKED else TILES)) + 16 * TILES

    def loaded_by(r, u):
        return r * (32 if u in PICKED else 16) + 16

    NB = NC - P
    assert NC % SLOTS == 0 and 0 < TP and TT <= TILES and 0 < NB < P

    def whole_chunks(edge_values):
        return edge_values[0:NC * CHUNK].rearrange("(c p j) -> c p j", p=P, j=TILES)

    def chunk_parts(edge_values):
        rows = edge_values[0:NC * CHUNK].rearrange("(c e) -> c e", e=CHUNK)
        return (rows[:, 0:PE_EDGES].rearrange("c (p j) -> c p j", p=P),
                rows[:, PE_EDGES:CHUNK].rearrange("c (p j) -> c p j", p=P))

    edge_rows = edge_attr[0:NC * CHUNK, :].rearrange("(c e) d -> c e d", e=CHUNK)
    edge_whole = edge_attr[0:NC * CHUNK, :].rearrange("(c p j) d -> c p (j d)", p=P, j=TILES)
    edge_parts = (edge_rows[:, 0:PE_EDGES, :].rearrange("c (p j) d -> c p (j d)", p=P),
                   edge_rows[:, PE_EDGES:CHUNK, :])
    src_whole, src_parts = whole_chunks(src), chunk_parts(src)
    dst_whole, dst_parts = whole_chunks(dst), chunk_parts(dst)
    src_rounds = src[0:NC * CHUNK].rearrange("(r u e) -> r u e", u=SLOTS,
                                             e=CHUNK)[:, PICKED[0]:PICKED[-1] + 1, PE_EDGES:CHUNK]
    T0, T1 = NC * CHUNK, NC * CHUNK + TW * P

    def tail_parts(edge_rows):
        return (edge_rows[T0:T1].rearrange("(p j) -> p j", p=P),
                edge_rows[T1:NE].rearrange("(p j) -> p j", p=TP))

    edge_tail = (edge_attr[T0:T1, :].rearrange("(p j) d -> p (j d)", p=P), edge_attr[T1:NE, :])
    dst_rows = dst[0:NC * CHUNK].rearrange("(c n) -> c n", n=CHUNK)
    dst_tail_row = dst[NC * CHUNK:NE].rearrange("(c n) -> c n", c=1)
    x_blocks = x[0:NFULL * W, :].rearrange("(b p) d -> p b d", p=W)
    out_blocks = out[0:NFULL * W, :].rearrange("(b p) d -> p b d", p=W)

    ctx = ExitStack()
    with ctx:
        def sb(name, shape, dt=fp32):
            return ctx.enter_context(nc.sbuf_tensor(name, shape, dt))

        def pb(name):
            return ctx.enter_context(nc.psum_tensor(name, [P, 512], fp32))

        def sem(name):
            return ctx.enter_context(nc.semaphore(name))

        def sems(name):
            return [sem(f"{name}{u}") for u in range(SLOTS)]

        src_all = sb("src_all", [P, NP, P], i32)
        src_low = sb("src_low", [P, NP, P], i32)
        src_start = sb("src_start", [P, NP, P], bf16)
        src_miss = sb("src_miss", [P, NP, P], bf16)
        onehot_src = [sb(f"onehot_src{k}", [P, b1 - b0, NP, P], bf16) for k, (b0, b1) in enumerate(PARTS)]
        picked_hm = sb("picked_hm", [P, NP * P])
        picked_l = sb("picked_l", [P, NP * P])
        srcs = [sb(f"srcs{u}", [P, TILES], i32) for u in range(SLOTS)]
        dsts = [sb(f"dsts{u}", [P, TILES], i32) for u in range(SLOTS)]
        gathered = [sb(f"gathered{u}", [P, TILES * D]) for u in range(SLOTS)]
        src_last = sb("src_last", [P, TT], i32)
        dst_last = sb("dst_last", [P, TT], i32)
        edges = [sb(f"edges{u}", [P, TILES * D]) for u in range(SLOTS)]
        gathered_T = [sb(f"gathered_T{u}", [P, PAIRS * P]) for u in range(SLOTS)]
        edges_T = [sb(f"edges_T{u}", [P, PAIRS * P]) for u in range(SLOTS)]
        messages = [sb(f"messages{u}", [P, TILES * D]) for u in range(SLOTS)]
        onehot = [sb(f"onehot{u}", [P, TILES, W]) for u in range(SLOTS)]

        XZ = sb("XZ", [P, NW * W + W])
        xb = sb("xb", [P, NW, D])
        x_hm = sb("x_hm", [P, NW, 2 * D], bf16)
        x_l = sb("x_l", [P, NW, D], bf16)
        block_start = sb("block_start", [P, NW, P], bf16)
        node_i = sb("node_i", [P, 1], i32)
        node = sb("node", [P, 1])
        ident = sb("ident", [P, P])
        count = sb("count", [P, W], i32)
        window_start = sb("window_start", [P, NW])
        window_start_i = sb("window_start_i", [P, NW], i32)
        ones = sb("ones", [1, P])
        ones_bf = sb("ones_bf", [P, P], bf16)
        m_stage = sb("m_stage", [D, 2, 2, D])
        u_stage = sb("u_stage", [D, 2 * D])
        w_gathered = sb("w_gathered", [P, 2 * D])
        w_stack = sb("w_stack", [P, D])
        w_edges = sb("w_edges", [P, 2 * D])
        w_update = sb("w_update", [P, D])
        bias = sb("bias", [P, 2, D])
        bias_rest = sb("bias_rest", [P, 2, 2, D])
        bias_split = sb("bias_split", [P, 3, 2, D], bf16)
        bias_parts = sb("bias_parts", [P, 2, TILES, D], bf16)
        dst_check = sb("dst_check", [P, 2, CHUNK], i32)
        dst_check_last = sb("dst_check_last", [1, TAIL], i32)
        least = sb("least", [P, 3])
        most = sb("most", [P, 3])
        span = sb("span", [P, 3])
        base_row = sb("base_row", [1, 2 * P])
        base_i = sb("base_i", [1, 2 * P], i32)
        base = sb("base", [P, 2 * P])
        widest = sb("widest", [1, 1])
        spread = sb("spread", [1, 1], i32)
        h = sb("h", [P, NW, D])
        sq = sb("sq", [P, NW, D])
        total = sb("total", [P, NW])
        var = sb("var", [P, NW])
        std = sb("std", [P, NW])
        eps_col = sb("eps_col", [P, 1])

        p_edges_T = pb("p_edges_T")
        p_gathered_T = pb("p_gathered_T")
        p_messages = [pb(f"p_messages{u}") for u in range(SLOTS)]
        p_dve = pb("p_dve")
        p_picked_hm = pb("p_picked_hm")
        p_picked_l = pb("p_picked_l")
        p_setup = p_picked_hm
        p_count = p_dve[:, 0:W]
        src_match = p_dve[:, W:W + NP * P // 2].bitcast(i32)
        p_windows = [p_messages[u][D:P, 0:W] for u in range(SLOTS)]

        s_ident = sem("s_ident")
        s_iota = sem("s_iota")
        s_cleared = sem("s_cleared")
        s_w_loaded = sem("s_w_loaded")
        s_bias_loaded = sem("s_bias_loaded")
        s_x_loaded = sem("s_x_loaded")
        s_x_rest_loaded = sem("s_x_rest_loaded")
        s_check_loaded = sem("s_check_loaded")
        s_last_cleared = sem("s_last_cleared")
        s_src_last_loaded = sem("s_src_last_loaded")
        s_dst_last_loaded = sem("s_dst_last_loaded")
        s_split = sem("s_split")
        s_w_T = sem("s_w_T")
        s_w_ready = sem("s_w_ready")
        s_x_T = sem("s_x_T")
        s_x_copied = sem("s_x_copied")
        s_least = sem("s_least")
        s_least_T = sem("s_least_T")
        s_base_row = sem("s_base_row")
        s_base_spread = sem("s_base_spread")
        s_base = sem("s_base")
        s_base_copied = sem("s_base_copied")
        s_dve = sem("s_dve")
        s_src_loaded = sems("s_src_loaded")
        s_dst_loaded = sems("s_dst_loaded")
        s_edges_loaded = sems("s_edges_loaded")
        s_gathered = sems("s_gathered")
        s_edges_T = sem("s_edges_T")
        s_edges_T_copied = sem("s_edges_T_copied")
        s_slot_taken = sem("s_slot_taken")
        s_gathered_T = sem("s_gathered_T")
        s_gathered_T_copied = sem("s_gathered_T_copied")
        s_summed = sem("s_summed")
        s_messages = sem("s_messages")
        s_onehot = sem("s_onehot")
        s_chunk_added = sem("s_chunk_added")
        s_window = sem("s_window")
        s_window_added = sem("s_window_added")
        s_round_src = sem("s_round_src")
        s_prep = sem("s_prep")
        s_onehot_src = sem("s_onehot_src")
        s_picked = sem("s_picked")
        s_picked_copied = sem("s_picked_copied")
        s_block_start = sem("s_block_start")
        s_x_rest = sem("s_x_rest")
        s_x_split = sem("s_x_split")
        s_update = sem("s_update")
        s_h = sem("s_h")
        s_centered = sem("s_centered")
        s_squared = sem("s_squared")
        s_var = sem("s_var")
        s_std = sem("s_std")
        s_scale = sem("s_scale")
        s_normed = sem("s_normed")
        s_out = sem("s_out")

        groups = [(b, min(b + FB, NW)) for b in range(0, NW, FB)]
        x_groups = [(b, min(b + XB, NW)) for b in range(0, NW, XB)]

        block = ctx.enter_context(nc.Block())

        @block.sync
        def _(sp):
            def load_src(chunk, u, picked=False):
                if picked:
                    sp.dma_start(srcs[u][:, 0:PT], src_parts[0][chunk]).then_inc(s_src_loaded[u], 16)
                else:
                    sp.dma_start(srcs[u][:, :], src_whole[chunk]).then_inc(s_src_loaded[u], 16)

            def load_dst(chunk, u, picked=False):
                if picked:
                    sp.dma_start(dsts[u][:, 0:PT], dst_parts[0][chunk]).then_inc(s_dst_loaded[u], 16)
                    sp.dma_start(dsts[u][:, PT:TILES], dst_parts[1][chunk]).then_inc(s_dst_loaded[u], 16)
                else:
                    sp.dma_start(dsts[u][:, :], dst_whole[chunk]).then_inc(s_dst_loaded[u], 16)

            def load_edges(chunk, u, picked=False):
                if picked:
                    sp.dma_start(edges[u][:, 0:PT * D], edge_parts[0][chunk]).then_inc(s_edges_loaded[u], 16)
                    sp.dma_start(edges[u][:, PT * D:TILES * D],
                                 edge_parts[1][chunk]).then_inc(s_edges_loaded[u], 16)
                else:
                    sp.dma_start(edges[u][:, :], edge_whole[chunk]).then_inc(s_edges_loaded[u], 16)

            def load_round_src(r):
                sp.dma_start(src_all[:, :, :], src_rounds[r].unsqueeze(0)
                             .to_broadcast([P, NP, P])).then_inc(s_round_src, 16)

            load_src(0, 0)
            sp.dma_start(m_stage[:, :, :, :], M_W.rearrange("o (h d) -> o h d", h=2).unsqueeze(2)
                         .to_broadcast([D, 2, 2, D])).then_inc(s_w_loaded, 16)
            load_src(1, 1)
            sp.dma_start(u_stage[:, :], U_W).then_inc(s_w_loaded, 16)
            load_edges(0, 0)
            load_src(2, 2)
            for k, b in enumerate((M_b, U_b)):
                sp.dma_start(bias[:, k, :], b.rearrange("(a d) -> a d", a=1)
                             .to_broadcast([P, D])).then_inc(s_bias_loaded, 16)
            load_dst(0, 0)
            for u in range(1, SLOTS):
                load_edges(u, u)
                load_dst(u, u)
            load_round_src(1)
            sp.wait_ge(s_last_cleared, 1)
            for tail, last, loaded in ((tail_parts(src), src_last, s_src_last_loaded),
                                       (tail_parts(dst), dst_last, s_dst_last_loaded)):
                sp.dma_start(last[:, 0:TW], tail[0]).then_inc(loaded, 16)
                sp.dma_start(last[0:TP, TW:TT], tail[1]).then_inc(loaded, 16)

            def load_chunk(r, u):
                chunk = r * SLOTS + u
                picked = u in PICKED
                sp.wait_ge(s_gathered[u], gathered_by(r - 1, u))
                load_src(chunk, u, picked)
                sp.wait_ge(s_edges_T, chunk - (SLOTS - 1))
                load_edges(chunk, u, picked)
                sp.wait_ge(s_chunk_added, chunk - (SLOTS - 1))
                load_dst(chunk, u, picked)

            with sp.Fori(1, ROUNDS - 1) as r:
                load_chunk(r, 0)
                sp.wait_ge(s_prep, r * 4)
                load_round_src(r + 1)
                for u in range(1, SLOTS):
                    load_chunk(r, u)
            for u in range(SLOTS):
                load_chunk(ROUNDS - 1, u)
            sp.wait_ge(s_edges_T, NC - (SLOTS - 1))
            sp.dma_start(edges[0][:, 0:TW * D], edge_tail[0]).then_inc(s_edges_loaded[0], 16)
            sp.dma_start(edges[0][0:TP, TW * D:TT * D], edge_tail[1]).then_inc(s_edges_loaded[0], 16)

            for g, (b0, b1) in enumerate(groups):
                sp.wait_ge(s_normed, g + 1)
                full = min(b1, NFULL)
                if full > b0:
                    sp.dma_start(out_blocks[:, b0:full, :], h[:, b0:full, :]).then_inc(s_out, 16)
                if b1 > NFULL:
                    sp.dma_start(out[NFULL * W:N, :], h[0:NLAST, NFULL, :]).then_inc(s_out, 16)
            stores = sum((min(b1, NFULL) > b0) + (b1 > NFULL) for b0, b1 in groups)
            sp.wait_ge(s_out, 16 * stores)

        @block.gpsimd
        def _(pool):
            nc.gpsimd.memset(ident[:, :], 0.0).then_inc(s_ident, 1)
            pool.wait_ge(s_ident, 1)
            nc.gpsimd.affine_select(out=ident[:, :], in_=ident[:, :], compare_op=ALU.not_equal, fill=1.0,
                                    base=0, pattern=[[-1, P]], channel_multiplier=1).then_inc(s_ident, 1)
            nc.gpsimd.iota(count[:, :], pattern=[[1, W]], base=0, channel_multiplier=0)
            nc.gpsimd.iota(window_start_i[:, :], pattern=[[W, NW]], base=0,
                           channel_multiplier=0)
            nc.gpsimd.iota(node_i[:, :], pattern=[[1, 1]], base=0, channel_multiplier=1).then_inc(s_iota, 1)

            def gather(u, index, tiles=TILES, last_parts=P):
                for j in range(tiles):
                    parts = last_parts if j == tiles - 1 else P
                    nc.gpsimd.indirect_dma_start(
                        out=gathered[u][0:parts, j * D:(j + 1) * D], out_offset=None, in_=x[:, :],
                        in_offset=bass.IndirectOffsetOnAxis(ap=index[0:parts, j:j + 1], axis=0),
                    ).then_inc(s_gathered[u], 16)

            for u in range(SLOTS):
                pool.wait_ge(s_src_loaded[u], 16)
                gather(u, srcs[u])
            with pool.Fori(1, ROUNDS) as r:
                for u in range(SLOTS):
                    pool.wait_ge(s_src_loaded[u], (r + 1) * 16)
                    pool.wait_ge(s_gathered_T, r * SLOTS + (u - SLOTS + 1))
                    pool.sem_inc(s_slot_taken, 1)
                    gather(u, srcs[u], PT if u in PICKED else TILES)
            pool.wait_ge(s_src_last_loaded, 2 * 16)
            pool.wait_ge(s_gathered_T, NC - SLOTS + 1)
            gather(0, src_last, TT, TP)

            for g, (b0, b1) in enumerate(groups):
                pool.wait_ge(s_scale, g + 1)
                nc.gpsimd.tensor_tensor(h[:, b0:b1, :], h[:, b0:b1, :],
                                        std[:, b0:b1].unsqueeze(2).to_broadcast([P, b1 - b0, D]),
                                        ALU.mult).then_inc(s_normed, 1)

        @block.scalar
        def _(act):
            act.dma_start(xb[:, 0:X_FIRST, :], x_blocks[:, 0:X_FIRST, :]).then_inc(s_x_loaded, 16)
            act.dma_start(dst_check[:, 0, :], dst_rows[0:P, :]).then_inc(s_check_loaded, 16)
            act.dma_start(dst_check[0:NB, 1, :], dst_rows[P:NC, :]).then_inc(s_check_loaded, 16)
            act.dma_start(dst_check_last[:, :], dst_tail_row).then_inc(s_check_loaded, 16)
            act.dma_start(xb[:, X_FIRST:NFULL, :], x_blocks[:, X_FIRST:NFULL, :]).then_inc(s_x_rest_loaded, 16)
            act.wait_ge(s_cleared, 1)
            act.dma_start(xb[0:NLAST, NFULL, :], x[NFULL * W:N, :]).then_inc(s_x_rest_loaded, 16)

            act.wait_ge(s_iota, 1)
            nc.scalar.copy(block_start[:, :, :],
                           window_start_i[:, :].unsqueeze(2).to_broadcast([P, NW, P])).then_inc(s_block_start, 1)

            def copy_x_T(g):
                b0, b1 = x_groups[g]
                act.wait_ge(s_x_T, g + 1)
                nc.scalar.copy(XZ[0:D, b0 * W:b1 * W],
                               p_messages[g % SLOTS][0:D, 0:(b1 - b0) * W]).then_inc(s_x_copied, 1)

            def copy_part(target, source):
                nc.scalar.copy(target, source).then_inc(s_x_split, 1)

            h0, h1 = slice(0, X_FIRST), slice(X_FIRST, NW)
            act.wait_ge(s_x_loaded, 16)
            copy_part(x_hm[:, h0, 0:D], xb[:, h0, :])
            for g in range(X_FIRST // XB):
                copy_x_T(g)
            act.wait_ge(s_x_rest, 1)
            copy_part(x_hm[:, h0, D:2 * D], sq[:, h0, :])
            act.wait_ge(s_x_rest_loaded, 2 * 16)
            copy_part(x_hm[:, h1, 0:D], xb[:, h1, :])
            for g in range(X_FIRST // XB, len(x_groups)):
                copy_x_T(g)
            act.wait_ge(s_x_rest, 2)
            copy_part(x_l[:, h0, :], sq[:, h0, :])
            act.wait_ge(s_x_rest, 3)
            copy_part(x_hm[:, h1, D:2 * D], sq[:, h1, :])
            act.wait_ge(s_x_rest, 4)
            copy_part(x_l[:, h1, :], sq[:, h1, :])

            def copy_edges_T(chunk, u, pairs=PAIRS):
                act.wait_ge(s_edges_T, chunk + 1)
                nc.scalar.copy(edges_T[u][:, 0:pairs * P], p_edges_T[:, 0:pairs * P]).then_inc(s_edges_T_copied, 1)

            def copy_gathered_T(chunk, u, pairs=PAIRS):
                act.wait_ge(s_gathered_T, chunk + 1)
                nc.scalar.copy(gathered_T[u][:, 0:pairs * P],
                               p_gathered_T[:, 0:pairs * P]).then_inc(s_gathered_T_copied, 1)

            def rectify(chunk, u, pairs=PAIRS):
                act.wait_ge(s_summed, chunk + 1)
                nc.scalar.activation(messages[u][:, 0:pairs * P], p_messages[u][:, 0:pairs * P],
                                     ACT.Relu).then_inc(s_messages, 1)

            copy_edges_T(0, 0)

            def chunk_steps(r, u):
                chunk = r * SLOTS + u
                copy_gathered_T(chunk, u)
                copy_edges_T(chunk + 1, (u + 1) % SLOTS)
                rectify(chunk, u)

            with act.Fori(0, ROUNDS - 1) as r:
                for u in range(SLOTS):
                    chunk_steps(r, u)
                act.wait_ge(s_picked, r + 1)
                nc.scalar.copy(picked_hm[:, :], p_picked_hm[:, 0:NP * P])
                nc.scalar.copy(picked_l[:, :], p_picked_l[:, 0:NP * P]).then_inc(s_picked_copied, 1)
            for u in range(SLOTS):
                chunk_steps(ROUNDS - 1, u)
            copy_gathered_T(NC, 0, TQ)
            rectify(NC, 0, TQ)

            def relu_update(g):
                b0, b1 = groups[g]
                act.wait_ge(s_update, g + 1)
                nc.scalar.activation(sq[:, b0:b1, :],
                                     p_messages[g % SLOTS][:, 0:(b1 - b0) * D].rearrange("p (b d) -> p b d", d=D),
                                     ACT.Relu).then_inc(s_h, 1)

            def square(g):
                b0, b1 = groups[g]
                act.wait_ge(s_centered, g + 1)
                nc.scalar.activation(sq[:, b0:b1, :], h[:, b0:b1, :], ACT.Square).then_inc(s_squared, 1)

            def root(g):
                b0, b1 = groups[g]
                act.wait_ge(s_var, g + 1)
                nc.scalar.activation(std[:, b0:b1], var[:, b0:b1], ACT.Sqrt, bias=eps_col[:, 0:1],
                                     scale=1.0 / D).then_inc(s_std, 1)

            for g in range(len(groups) + 2):
                if g < len(groups):
                    relu_update(g)
                if 1 <= g <= len(groups):
                    square(g - 1)
                if g >= 2:
                    root(g - 2)

        @block.vector
        def _(dve):
            chain = [0]

            def link(ins):
                chain[0] += 1
                ins.then_inc(s_dve, 1)
                dve.wait_ge(s_dve, chain[0])

            nc.vector.memset(xb[:, NFULL, :], 0.0).then_inc(s_cleared, 1)
            nc.vector.memset(dst_last[:, :], -1).then_inc(s_last_cleared, 1)
            nc.vector.memset(ones[:, :], 1.0)
            nc.vector.memset(ones_bf[:, :], 1.0)
            nc.vector.memset(eps_col[:, :], EPS)
            nc.vector.memset(bias_parts[:, :, :, :], 0.0)
            nc.vector.memset(XZ[D:P, :], 0.0)
            nc.vector.memset(w_gathered[:, :], 0.0)
            link(nc.vector.memset(w_edges[:, :], 0.0))
            dve.wait_ge(s_iota, 1)
            nc.vector.tensor_copy(p_count, count[:, :])
            nc.vector.tensor_copy(node[:, :], node_i[:, :])
            nc.vector.tensor_copy(window_start[:, :], window_start_i[:, :])
            h0, h1 = slice(0, X_FIRST), slice(X_FIRST, NW)

            def first_rest(half, part):
                dve.wait_ge(s_x_split, part)
                nc.vector.tensor_tensor(sq[:, half, :], xb[:, half, :], x_hm[:, half, 0:D],
                                        ALU.subtract).then_inc(s_x_rest, 1)

            def second_rest(half, part):
                dve.wait_ge(s_x_split, part)
                nc.vector.tensor_tensor(sq[:, half, :], sq[:, half, :], x_hm[:, half, D:2 * D],
                                        ALU.subtract).then_inc(s_x_rest, 1)

            dve.wait_ge(s_w_T, 1)
            nc.vector.tensor_copy(w_gathered[0:D, 0:D], p_setup[0:D, 0:D])
            nc.vector.tensor_copy(w_gathered[D:P, D:2 * D], p_setup[D:P, 0:D])
            nc.vector.tensor_copy(w_stack[:, :], p_setup[:, 0:D])
            nc.vector.tensor_copy(w_edges[0:D, 0:D], p_setup[0:D, D:2 * D])
            nc.vector.tensor_copy(w_edges[D:P, D:2 * D], p_setup[D:P, D:2 * D])
            nc.vector.tensor_copy(w_update[:, :], p_setup[:, 2 * D:3 * D]).then_inc(s_w_ready, 1)
            first_rest(h0, 1)
            dve.wait_ge(s_check_loaded, 3 * 16)
            for k, n, rows in ((0, P, dst_check[:, 0, :]), (1, NB, dst_check[0:NB, 1, :]),
                               (2, 1, dst_check_last[:, :])):
                nc.vector.tensor_reduce(least[0:n, k:k + 1], rows, AX.X, ALU.min)
                link(nc.vector.tensor_reduce(most[0:n, k:k + 1], rows, AX.X, ALU.max))
                last = nc.vector.tensor_tensor(span[0:n, k:k + 1], most[0:n, k:k + 1], least[0:n, k:k + 1],
                                               ALU.subtract)
            last.then_inc(s_least, 1)
            dve.wait_ge(s_bias_loaded, 2 * 16)
            rest = bias[:, :, :]
            for k in range(3):
                link(nc.vector.tensor_copy(bias_split[:, k, :, :], rest))
                if k < 2:
                    link(nc.vector.tensor_tensor(bias_rest[:, k, :, :], rest, bias_split[:, k, :, :],
                                                 ALU.subtract))
                    rest = bias_rest[:, k, :, :]
                q = 32 * k
                last = nc.vector.tensor_copy(bias_parts[q:q + 1, :, :, :], bias_split[q:q + 1, k, :, :]
                                             .unsqueeze(2).to_broadcast([1, 2, TILES, D]))
            last.then_inc(s_split, 1)
            dve.wait_ge(s_least_T, 1)
            nc.vector.tensor_copy(base_row[:, 0:NC], p_setup[0:1, 0:NC])
            nc.vector.tensor_copy(base_row[:, NC:NC + 1], least[0:1, 2:3]).then_inc(s_base_row, 1)
            nc.vector.tensor_copy(base_i[:, 0:NC], p_setup[0:1, 0:NC])
            nc.vector.tensor_copy(base_i[:, NC:NC + 1], least[0:1, 2:3])
            link(nc.vector.reduce_max(widest[:, :], p_setup[0:1, 2 * P:2 * P + NC], AX.X))
            link(nc.vector.tensor_tensor(widest[:, :], widest[:, :], span[0:1, 2:3], ALU.max))
            nc.vector.tensor_scalar(spread[:, :], widest[:, :], float(W), None, ALU.is_ge).then_inc(s_base, 1)
            dve.wait_ge(s_base_spread, 1)
            nc.vector.tensor_copy(base[:, 0:NC + 1], p_gathered_T[:, 0:NC + 1]).then_inc(s_base_copied, 1)
            dve.wait_ge(s_base_copied, 1)
            dve.wait_ge(s_base, 1)
            dve.wait_ge(s_block_start, 1)

            second_rest(h0, 2)
            first_rest(h1, 3)
            second_rest(h1, 5)

            count_b = p_count.unsqueeze(1).to_broadcast([P, TILES, W])

            def compare(u, start, nodes, tiles):
                nc.vector.scalar_tensor_tensor(
                    out=onehot[u][:, 0:tiles, :], in0=count_b[:, 0:tiles, :], scalar=start,
                    in1=nodes[:, :].unsqueeze(2).to_broadcast([P, tiles, W]),
                    op0=ALU.add, op1=ALU.is_equal).then_inc(s_onehot, 1)

            def match_src(r):
                dve.wait_ge(s_round_src, (r + 1) * 16)
                nc.vector.tensor_scalar(src_low[:, :, :], src_all[:, :, :], P - 1, None,
                                        ALU.bitwise_and).then_inc(s_prep, 1)
                dve.wait_ge(s_prep, r * 4 + 1)
                nc.vector.scalar_tensor_tensor(out=src_start[:, :, :], in0=src_low[:, :, :], scalar=-1.0,
                                               in1=src_all[:, :, :], op0=ALU.mult, op1=ALU.add)
                nc.vector.tensor_scalar(src_miss[:, :, :], src_low[:, :, :], node[:, 0:1], MISS,
                                        ALU.not_equal, ALU.mult).then_inc(s_prep, 1)
                dve.wait_ge(s_prep, r * 4 + 2)
                nc.vector.tensor_tensor(src_start[:, :, :], src_start[:, :, :], src_miss[:, :, :],
                                        ALU.add).then_inc(s_prep, 1)
                dve.wait_ge(s_prep, r * 4 + 3)
                nc.vector.tensor_scalar(src_match, src_start[:, :, :].rearrange("p u e -> p (u e)").bitcast(i32),
                                        0, None, ALU.bitwise_or).then_inc(s_prep, 1)
                dve.wait_ge(s_prep, r * 4 + 4)

            def compare_src(k):
                b0, b1 = PARTS[k]
                for u in range(NP):
                    match = src_match.bitcast(bf16)[:, u * P:(u + 1) * P]
                    last = nc.vector.tensor_tensor(onehot_src[k][:, :, u, :],
                                                   match.unsqueeze(1).to_broadcast([P, b1 - b0, P]),
                                                   block_start[:, b0:b1, :], ALU.is_equal)
                last.then_inc(s_onehot_src, 1)

            def pick(r, u):
                if u == 0:
                    match_src(r)
                compare_src(u)

            def one_window(chunk, u, nodes, loaded, loaded_count, tiles=TILES, picks=None):
                dve.wait_ge(loaded, loaded_count)
                compare(u, base[:, bass.ds(chunk, 1)], nodes, tiles)
                if picks is not None:
                    pick(picks, u)
                start = dve.value_load(base_i[0:1, bass.ds(chunk, 1)], min_val=0, max_val=N - 1)
                dve.wait_ge(s_window, chunk + 1)
                columns = XZ[D:P, bass.ds(start, W)]
                nc.vector.tensor_tensor(columns, columns, p_windows[u],
                                        ALU.add).then_inc(s_chunk_added, 1)

            def all_windows(chunk, u, nodes, loaded, loaded_count, tiles=TILES, picks=None):
                if picks is not None:
                    pick(picks, u)
                with dve.Fori(0, NW) as w:
                    dve.wait_ge(loaded, loaded_count)
                    compare(u, window_start[:, bass.ds(w, 1)], nodes, tiles)
                    dve.wait_ge(s_window, chunk * NW + w + 1)
                    columns = XZ[D:P, bass.ds(w * W, W)]
                    nc.vector.tensor_tensor(columns, columns, p_windows[u],
                                            ALU.add).then_inc(s_window_added, 1)
                dve.wait_ge(s_window_added, (chunk + 1) * NW)
                dve.sem_inc(s_chunk_added, 1)

            def chunks(windows):
                with dve.Fori(0, ROUNDS - 1) as r:
                    for u in range(SLOTS):
                        windows(r * SLOTS + u, u, dsts[u], s_dst_loaded[u], loaded_by(r, u), picks=r)
                for u in range(SLOTS):
                    windows(NC - SLOTS + u, u, dsts[u], s_dst_loaded[u],
                            loaded_by(ROUNDS - 1, u))
                windows(NC, 0, dst_last, s_dst_last_loaded, 2 * 16, TT)

            is_spread = dve.value_load(spread[0:1, 0:1], min_val=0, max_val=1)
            with dve.If(is_spread == 0):
                chunks(one_window)
            with dve.Else():
                chunks(all_windows)

            def center(g):
                b0, b1 = groups[g]
                n = b1 - b0
                hg = h[:, b0:b1, :]
                dve.wait_ge(s_h, g + 1)
                link(nc.vector.tensor_tensor(hg, sq[:, b0:b1, :], xb[:, b0:b1, :], ALU.add))
                link(nc.vector.reduce_sum(total[:, b0:b1], hg, AX.X))
                nc.vector.scalar_tensor_tensor(out=hg, in0=total[:, b0:b1].unsqueeze(2).to_broadcast([P, n, D]),
                                               scalar=-1.0 / D, in1=hg, op0=ALU.mult,
                                               op1=ALU.add).then_inc(s_centered, 1)

            def sum_squares(g):
                b0, b1 = groups[g]
                dve.wait_ge(s_squared, g + 1)
                nc.vector.reduce_sum(var[:, b0:b1], sq[:, b0:b1, :], AX.X).then_inc(s_var, 1)

            def invert(g):
                b0, b1 = groups[g]
                dve.wait_ge(s_std, g + 1)
                nc.vector.reciprocal(std[:, b0:b1], std[:, b0:b1]).then_inc(s_scale, 1)

            for g in range(len(groups) + 2):
                if g < len(groups):
                    center(g)
                if 1 <= g <= len(groups):
                    sum_squares(g - 1)
                if g >= 2:
                    invert(g - 2)

        @block.tensor
        def _(pe):
            def spread_base():
                pe.wait_ge(s_least, 1)
                pe.wait_ge(s_w_ready, 1)
                for k, n in ((0, P), (1, NB)):
                    nc.tensor.transpose(p_setup[0:1, k * P:k * P + n], least[0:n, k:k + 1], ident[0:n, 0:n])
                    last = nc.tensor.transpose(p_setup[0:1, (2 + k) * P:(2 + k) * P + n], span[0:n, k:k + 1],
                                               ident[0:n, 0:n])
                last.then_inc(s_least_T, 1)
                pe.wait_ge(s_base_row, 1)
                nc.tensor.matmul(p_gathered_T[:, 0:NC + 1], ones[0:1, :], base_row[0:1, 0:NC + 1],
                                 start=True, stop=True).then_inc(s_base_spread, 1)

            pe.wait_ge(s_ident, 2)
            pe.wait_ge(s_w_loaded, 2 * 16)
            for k, w in enumerate((m_stage[:, 0, :, :].rearrange("o t d -> o (t d)"),
                                   m_stage[:, 1, :, :].rearrange("o t d -> o (t d)"), u_stage[:, :])):
                last = nc.tensor.transpose(p_setup[:, k * D:(k + 1) * D], w, ident[0:D, 0:D])
            last.then_inc(s_w_T, 1)
            pe.wait_ge(s_x_loaded, 16)
            for g, (b0, b1) in enumerate(x_groups):
                if b0 == X_FIRST:
                    pe.wait_ge(s_x_rest_loaded, 2 * 16)
                if g >= SLOTS:
                    pe.wait_ge(s_x_copied, g - SLOTS + 1)
                for b in range(b0, b1):
                    last = nc.tensor.transpose(p_messages[g % SLOTS][0:D, (b - b0) * W:(b - b0 + 1) * W],
                                               xb[:, b, :], ident[:, :])
                last.then_inc(s_x_T, 1)
            spread_base()
            pe.wait_ge(s_x_copied, len(x_groups))
            pe.wait_ge(s_split, 1)
            pe.wait_ge(s_base_copied, 1)

            def add_bias(p, k, tiles):
                nc.tensor.matmul(p[:, 0:tiles * D], ones_bf[:, :],
                                 bias_parts[:, k, 0:tiles, :].rearrange("p t d -> p (t d)"),
                                 start=True, stop=False)

            def transpose_edges(u, edges_count, pairs=PAIRS):
                pe.wait_ge(s_edges_loaded[u], edges_count)
                for q in range(pairs):
                    last = nc.tensor.transpose(p_edges_T[:, q * P:(q + 1) * P], edges[u][:, q * P:(q + 1) * P],
                                               ident[:, :])
                last.then_inc(s_edges_T, 1)

            def add_edges(chunk, u, pairs=PAIRS):
                add_bias(p_messages[u], 0, 2 * pairs)
                pe.wait_ge(s_edges_T_copied, chunk + 1)
                for q in range(pairs):
                    nc.tensor.matmul(p_messages[u][:, q * P:(q + 1) * P], edges_T[u][:, q * P:(q + 1) * P],
                                     w_edges[:, :], start=False, stop=False)

            def transpose_gathered(u, gathered_count, tiles=TILES):
                pe.wait_ge(s_gathered[u], gathered_count)
                for q in range(0, tiles, 2):
                    rows = min(tiles - q, 2) * D
                    last = nc.tensor.transpose(p_gathered_T[0:rows, q * D:q * D + P],
                                               gathered[u][:, q * D:q * D + rows], ident[:, :])
                last.then_inc(s_gathered_T, 1)

            def add_gathered(chunk, u, pairs=PAIRS):
                pe.wait_ge(s_gathered_T_copied, chunk + 1)
                for q in range(pairs):
                    last = nc.tensor.matmul(p_messages[u][:, q * P:(q + 1) * P],
                                            gathered_T[u][:, q * P:(q + 1) * P], w_gathered[:, :],
                                            start=False, stop=(q == pairs - 1))
                last.then_inc(s_summed, 1)

            def add_picked(chunk, u):
                for rows in (picked_hm, picked_l):
                    nc.tensor.matmul(p_messages[u][:, PT * D:TILES * D], rows[:, PICKED.index(u) * P:(PICKED.index(u) + 1) * P],
                                     w_stack[:, :], start=False, stop=False)
                pe.wait_ge(s_gathered_T_copied, chunk + 1)
                for q in range(PAIRS - 1):
                    nc.tensor.matmul(p_messages[u][:, q * P:(q + 1) * P], gathered_T[u][:, q * P:(q + 1) * P],
                                     w_gathered[:, :], start=False, stop=False)
                q = PAIRS - 1
                nc.tensor.matmul(p_messages[u][:, q * P:q * P + D], gathered_T[u][0:D, q * P:(q + 1) * P],
                                 w_stack[0:D, :], start=False, stop=True).then_inc(s_summed, 1)

            def pick(chunk, k):
                pe.wait_ge(s_onehot_src, chunk + 1)
                b0, b1 = PARTS[k]

                def edges_of(b):
                    return onehot_src[k][:, b - b0, :, :].rearrange("p u e -> p (u e)")

                for b in range(b0, b1, 2):
                    pair = range(b, min(b + 2, b1))
                    for c in pair:
                        nc.tensor.matmul(p_picked_hm[:, 0:NP * P], x_hm[:, c, :], edges_of(c),
                                         start=(c == 0), stop=(c == NW - 1))
                    for c in pair:
                        half = (c - b) * D
                        last = nc.tensor.matmul(p_picked_l[half:half + D, 0:NP * P], x_l[:, c, :], edges_of(c),
                                                start=(c < 2), stop=(c >= NW - 2))
                if k == len(PARTS) - 1:
                    last.then_inc(s_picked, 1)

            def sum_window(u, tiles):
                for j in range(tiles):
                    last = nc.tensor.matmul(p_windows[u], messages[u][:, j * D:(j + 1) * D],
                                            onehot[u][:, j, :], start=(j == 0), stop=(j == tiles - 1))
                last.then_inc(s_window, 1)

            def one_window(chunk, u, tiles=TILES):
                pe.wait_ge(s_messages, chunk + 1)
                pe.wait_ge(s_onehot, chunk + 1)
                sum_window(u, tiles)

            def all_windows(chunk, u, tiles=TILES):
                with pe.Fori(0, NW) as w:
                    pe.wait_ge(s_messages, chunk + 1)
                    pe.wait_ge(s_onehot, chunk * NW + w + 1)
                    sum_window(u, tiles)

            def chunks(windows):
                transpose_edges(0, loaded_by(0, 0))
                add_edges(0, 0)
                for u in range(SLOTS):
                    v = (u + 1) % SLOTS
                    transpose_gathered(u, 16 * TILES)
                    transpose_edges(v, loaded_by(1 if v == 0 else 0, v))
                    add_gathered(u, u)
                    add_edges(u + 1, v)
                    windows(u, u)
                    if u == 0:
                        pe.wait_ge(s_x_split, 6)
                    pick(u, u)
                with pe.Fori(1, ROUNDS - 1) as r:
                    for u in range(SLOTS):
                        chunk, v = r * SLOTS + u, (u + 1) % SLOTS
                        transpose_gathered(u, gathered_by(r, u), PT if u in PICKED else TILES)
                        transpose_edges(v, loaded_by(r + 1 if v == 0 else r, v))
                        if u == PICKED[0]:
                            pe.wait_ge(s_picked_copied, r)
                        (add_picked if u in PICKED else add_gathered)(chunk, u)
                        add_edges(chunk + 1, v)
                        windows(chunk, u)
                        pick(chunk, u)
                pe.wait_ge(s_picked_copied, ROUNDS - 1)
                for u in range(SLOTS):
                    chunk, v = (ROUNDS - 1) * SLOTS + u, (u + 1) % SLOTS
                    last = u == SLOTS - 1
                    transpose_gathered(u, gathered_by(ROUNDS - 1, u), PT if u in PICKED else TILES)
                    transpose_edges(v, loaded_by(ROUNDS - 1, v) + (32 if last else 0), TQ if last else PAIRS)
                    (add_picked if u in PICKED else add_gathered)(chunk, u)
                    add_edges(chunk + 1, v, TQ if last else PAIRS)
                    windows(chunk, u)
                transpose_gathered(0, gathered_by(ROUNDS - 1, 0) + TT * 16, 2 * TQ)
                add_gathered(NC, 0, TQ)
                windows(NC, 0, TT)

            pe.wait_ge(s_base, 1)
            is_spread = pe.value_load(spread[0:1, 0:1], min_val=0, max_val=1)
            with pe.If(is_spread == 0):
                chunks(one_window)
            with pe.Else():
                chunks(all_windows)

            pe.wait_ge(s_chunk_added, NC + 1)
            for g, (b0, b1) in enumerate(groups):
                if g >= SLOTS:
                    pe.wait_ge(s_h, g - SLOTS + 1)
                add_bias(p_messages[g % SLOTS], 1, b1 - b0)
                for b in range(b0, b1):
                    last = nc.tensor.matmul(p_messages[g % SLOTS][:, (b - b0) * D:(b - b0 + 1) * D],
                                            XZ[:, b * W:(b + 1) * W], w_update[:, :],
                                            start=False, stop=(b == b1 - 1))
                last.then_inc(s_update, 1)


_INS = ['x', 'src', 'dst', 'edge_attr_64', 'L0_gnn_M_W', 'L0_gnn_M_b', 'L0_gnn_U_W', 'L0_gnn_U_b']
_OUTS = [((6250, 64), 'float32')]


def kernel(**inputs):
    import numpy as _np
    import concourse.bacc as _bacc
    from concourse import mybir as _mybir
    from concourse.bass_utils import run_bass_kernel_spmd as _run

    nc = _bacc.Bacc("TRN2", target_bir_lowering=False, num_devices=1)
    arrays, args = {}, []
    for name in _INS:
        a = _np.ascontiguousarray(inputs[name])
        arrays[f"in_{name}_dram"] = a
        args.append(nc.dram_tensor(f"in_{name}_dram", a.shape, _mybir.dt.from_np(a.dtype), kind="ExternalInput").ap())
    for i, (shape, dtype) in enumerate(_OUTS):
        dt = _mybir.dt.from_np(_np.dtype(dtype))
        args.append(nc.dram_tensor(f"out_{i}_dram", shape, dt, kind="ExternalOutput").ap())
    gnn_residual_layernorm_kernel(nc, *args)
    r = _run(nc, [arrays], core_ids=[0])
    return r.results[0]["out_0_dram"]
```

```python
import numpy as np
import concourse.bass as bass
from concourse import mybir
from contextlib import ExitStack


def gnn_residual_layernorm_kernel(
    nc: bass.Bass,
    x: bass.AP,
    src: bass.AP,
    dst: bass.AP,
    edge_attr: bass.AP,
    M_W: bass.AP,
    M_b: bass.AP,
    U_W: bass.AP,
    U_b: bass.AP,
    out: bass.AP,
):
    fp32 = mybir.dt.float32
    bf16 = mybir.dt.bfloat16
    i32 = mybir.dt.int32
    ALU = mybir.AluOpType
    ACT = mybir.ActivationFunctionType
    AX = mybir.AxisListType

    P = 128
    N, D = x.shape
    NE = src.shape[0]
    TILES = 8
    PAIRS = TILES // 2
    CHUNK = TILES * P
    NC = NE // CHUNK
    TAIL = NE - NC * CHUNK
    TW = TAIL // P
    TP = TAIL - TW * P
    TT = TW + 1
    TQ = -(-TT // 2)
    SLOTS = 3
    PT = TILES - 1
    PE_EDGES = PT * P
    ROUNDS = NC // SLOTS
    W = 128
    NW = -(-N // W)
    NFULL = N // W
    NLAST = N - NFULL * W
    MISS = 8192.0
    assert N <= MISS and P == 128
    PARTS = [(0, 17), (17, 33), (33, NW)]
    FB = 8
    XB = 4
    X_FIRST = NFULL // 2 // FB * FB
    LAG = 2
    EPS = 1e-5

    FIRST_PICKED = 2

    def gathered_by(r):
        if isinstance(r, int) and r < FIRST_PICKED:
            return (r + 1) * 16 * TILES
        return r * (16 * PT) + 16 * (FIRST_PICKED * TILES - (FIRST_PICKED - 1) * PT)

    def loaded_by(r):
        if isinstance(r, int) and r < FIRST_PICKED:
            return (r + 1) * 16
        return r * 32 - (FIRST_PICKED - 2) * 16

    NB = NC - P
    assert NC % SLOTS == 0 and 0 < TP and TT <= TILES and 0 < NB < P

    def whole_chunks(edge_values):
        return edge_values[0:NC * CHUNK].rearrange("(c p j) -> c p j", p=P, j=TILES)

    def chunk_parts(edge_values):
        rows = edge_values[0:NC * CHUNK].rearrange("(c e) -> c e", e=CHUNK)
        return (rows[:, 0:PE_EDGES].rearrange("c (p j) -> c p j", p=P),
                rows[:, PE_EDGES:CHUNK].rearrange("c (p j) -> c p j", p=P))

    edge_rows = edge_attr[0:NC * CHUNK, :].rearrange("(c e) d -> c e d", e=CHUNK)
    edge_whole = edge_attr[0:NC * CHUNK, :].rearrange("(c p j) d -> c p (j d)", p=P, j=TILES)
    edge_parts = (edge_rows[:, 0:PE_EDGES, :].rearrange("c (p j) d -> c p (j d)", p=P),
                  edge_rows[:, PE_EDGES:CHUNK, :])
    src_whole, src_parts = whole_chunks(src), chunk_parts(src)
    dst_whole, dst_parts = whole_chunks(dst), chunk_parts(dst)
    src_rounds = src[0:NC * CHUNK].rearrange("(r u e) -> r u e", u=SLOTS,
                                             e=CHUNK)[:, :, PE_EDGES:CHUNK]
    T0, T1 = NC * CHUNK, NC * CHUNK + TW * P

    def tail_parts(edge_values):
        return (edge_values[T0:T1].rearrange("(p j) -> p j", p=P),
                edge_values[T1:NE].rearrange("(p j) -> p j", p=TP))

    edge_tail = (edge_attr[T0:T1, :].rearrange("(p j) d -> p (j d)", p=P), edge_attr[T1:NE, :])
    dst_rows = dst[0:NC * CHUNK].rearrange("(c n) -> c n", n=CHUNK)
    dst_tail_row = dst[NC * CHUNK:NE].rearrange("(c n) -> c n", c=1)
    x_blocks = x[0:NFULL * W, :].rearrange("(b p) d -> p b d", p=W)
    out_blocks = out[0:NFULL * W, :].rearrange("(b p) d -> p b d", p=W)

    ctx = ExitStack()
    with ctx:
        def sb(name, shape, dt=fp32):
            return ctx.enter_context(nc.sbuf_tensor(name, shape, dt))

        def pb(name):
            return ctx.enter_context(nc.psum_tensor(name, [P, 512], fp32))

        Y_rows = nc.dram_tensor("Y_rows", [N, D], fp32, kind="Internal").ap()
        Y_blocks = Y_rows[0:NFULL * W, :].rearrange("(b p) d -> p b d", p=W)

        def sem(name):
            return ctx.enter_context(nc.semaphore(name))

        def sems(name):
            return [sem(f"{name}{u}") for u in range(SLOTS)]

        src_all = sb("src_all", [P, SLOTS, P], i32)
        src_low = sb("src_low", [P, SLOTS, P], i32)
        src_start = sb("src_start", [P, SLOTS, P], bf16)
        src_miss = sb("src_miss", [P, SLOTS, P], bf16)
        onehot_src = [sb(f"onehot_src{k}", [P, b1 - b0, SLOTS, P], bf16) for k, (b0, b1) in enumerate(PARTS)]
        picked_hm = sb("picked_hm", [P, SLOTS * P])
        picked_l = sb("picked_l", [P, SLOTS * P])
        srcs = [sb(f"srcs{u}", [P, TILES], i32) for u in range(SLOTS)]
        dsts = [sb(f"dsts{u}", [P, TILES], i32) for u in range(SLOTS)]
        gathered = [sb(f"gathered{u}", [P, TILES * D]) for u in range(SLOTS)]
        x_rows = [sb(f"x_rows{u}", [P, TILES * D]) for u in range(SLOTS)]
        x_rows_T = sb("x_rows_T", [P, PAIRS * P])
        src_last = sb("src_last", [P, TT], i32)
        dst_last = sb("dst_last", [P, TT], i32)
        edges = [sb(f"edges{u}", [P, TILES * D]) for u in range(SLOTS)]
        edges_T = [sb(f"edges_T{u}", [P, PAIRS * P]) for u in range(SLOTS)]
        messages = [sb(f"messages{u}", [P, TILES * D]) for u in range(SLOTS)]
        onehot = [sb(f"onehot{u}", [P, TILES, W]) for u in range(SLOTS)]

        XZ = sb("XZ", [P, NW * W + W])
        x_pairs_T = sb("x_pairs_T", [P, -(-NW // 2) * W])
        xb = sb("xb", [P, NW, D])
        Y_hm = sb("Y_hm", [P, NW, 2 * D], bf16)
        Y_l = sb("Y_l", [P, NW, D], bf16)
        block_start = sb("block_start", [P, NW, P], bf16)
        node_i = sb("node_i", [P, 1], i32)
        node = sb("node", [P, 1])
        ident = sb("ident", [P, P])
        count = sb("count", [P, W], i32)
        window_start = sb("window_start", [P, NW])
        window_start_i = sb("window_start_i", [P, NW], i32)
        ones = sb("ones", [1, P])
        m_stage = sb("m_stage", [D, 2, 2, D])
        u_stage = sb("u_stage", [D, 2 * D])
        w_gathered = sb("w_gathered", [P, 2 * D])
        ident_stack = sb("ident_stack", [P, D])
        w_edges = sb("w_edges", [P, 2 * D])
        w_update = sb("w_update", [P, D])
        m_bias = sb("m_bias", [P, 1, D])
        u_bias = sb("u_bias", [D, 1])
        dst_check = [onehot[k][:, :, :].rearrange("p t w -> p (t w)").bitcast(i32) for k in (1, 2)]
        dst_check_last = sb("dst_check_last", [1, TAIL], i32)
        least = sb("least", [P, 3])
        most = sb("most", [P, 3])
        span = sb("span", [P, 3])
        base_row = sb("base_row", [1, 2 * P])
        base_i = sb("base_i", [1, 2 * P], i32)
        base = sb("base", [P, 2 * P])
        widest = sb("widest", [1, 1])
        spread = sb("spread", [1, 1], i32)
        Y = sb("Y", [P, NW, D])
        h = Y
        sq = sb("sq", [P, NW, D])
        update_T = [onehot[k][0:D, 0:XB, :].rearrange("p t w -> p (t w)") for k in range(SLOTS)]
        total = sb("total", [P, NW])
        mean = sb("mean", [P, NW])
        var = sb("var", [P, NW])
        std = sb("std", [P, NW])
        eps_col = sb("eps_col", [P, 1])

        p_edges_T = pb("p_edges_T")
        p_base = pb("p_base")
        p_Y = [p_edges_T, p_base]
        p_messages = [pb(f"p_messages{u}") for u in range(SLOTS)]
        p_dve = pb("p_dve")
        p_picked_hm = pb("p_picked_hm")
        p_picked_l = pb("p_picked_l")
        p_setup = p_picked_hm
        p_x_rows_T = p_base
        p_update_T = p_messages
        p_update = p_Y
        p_count = p_dve[:, 0:W]
        src_match = p_dve[:, W:W + SLOTS * P // 2].bitcast(i32)
        p_windows = [p_messages[u][D:P, 0:W] for u in range(SLOTS)]

        s_ident = sem("s_ident")
        s_iota = sem("s_iota")
        s_cleared = sem("s_cleared")
        s_eps = sem("s_eps")
        s_w_loaded = sem("s_w_loaded")
        s_bias_loaded = sem("s_bias_loaded")
        s_x_loaded = sem("s_x_loaded")
        s_x_more_loaded = sem("s_x_more_loaded")
        s_x_rest_loaded = sem("s_x_rest_loaded")
        s_check_loaded = sem("s_check_loaded")
        s_check_more_loaded = sem("s_check_more_loaded")
        s_last_cleared = sem("s_last_cleared")
        s_src_last_loaded = sem("s_src_last_loaded")
        s_dst_last_loaded = sem("s_dst_last_loaded")
        s_w_T = sem("s_w_T")
        s_w_ready = sem("s_w_ready")
        s_x_T = sem("s_x_T")
        s_x_copied = sem("s_x_copied")
        s_XZ = sem("s_XZ")
        s_least = sem("s_least")
        s_least_T = sem("s_least_T")
        s_base_row = sem("s_base_row")
        s_base_spread = sem("s_base_spread")
        s_base = sem("s_base")
        s_base_copied = sem("s_base_copied")
        s_dve = sem("s_dve")
        s_src_loaded = sems("s_src_loaded")
        s_dst_loaded = sems("s_dst_loaded")
        s_edges_loaded = sems("s_edges_loaded")
        s_gathered = sems("s_gathered")
        s_edges_T = sem("s_edges_T")
        s_edges_T_copied = sem("s_edges_T_copied")
        s_slot_taken = sem("s_slot_taken")
        s_x_rows_T = sem("s_x_rows_T")
        s_x_rows_T_copied = sem("s_x_rows_T_copied")
        s_rows_added = sem("s_rows_added")
        s_summed = sem("s_summed")
        s_messages = sem("s_messages")
        s_onehot = sem("s_onehot")
        s_chunk_added = sem("s_chunk_added")
        s_window = sem("s_window")
        s_window_added = sem("s_window_added")
        s_round_src = sem("s_round_src")
        s_prep = sem("s_prep")
        s_onehot_src = sem("s_onehot_src")
        s_picked = sem("s_picked")
        s_picked_copied = sem("s_picked_copied")
        s_block_start = sem("s_block_start")
        s_Y_rest = sem("s_Y_rest")
        s_Y_summed = sem("s_Y_summed")
        s_Y = sem("s_Y")
        s_Y_stored = sem("s_Y_stored")
        s_Y_split = sem("s_Y_split")
        s_update_T = sem("s_update_T")
        s_update_relu = sem("s_update_relu")
        s_update = sem("s_update")
        s_h = sem("s_h")
        s_mean = sem("s_mean")
        s_centered = sem("s_centered")
        s_squared = sem("s_squared")
        s_var = sem("s_var")
        s_std = sem("s_std")
        s_scale = sem("s_scale")
        s_normed = sem("s_normed")
        s_out = sem("s_out")

        groups = [(b, min(b + FB, NW)) for b in range(0, NW, FB)]
        stores = sum((min(b1, NFULL) > b0) + (b1 > NFULL) for b0, b1 in groups)
        x_groups = [(b, min(b + XB, NW)) for b in range(0, NW, XB)]

        block = ctx.enter_context(nc.Block())

        @block.sync
        def _(sp):
            def load_src(chunk, u, picked=False):
                if picked:
                    sp.dma_start(srcs[u][:, 0:PT], src_parts[0][chunk]).then_inc(s_src_loaded[u], 16)
                else:
                    sp.dma_start(srcs[u][:, :], src_whole[chunk]).then_inc(s_src_loaded[u], 16)

            def load_dst(chunk, u, picked=False):
                if picked:
                    sp.dma_start(dsts[u][:, 0:PT], dst_parts[0][chunk]).then_inc(s_dst_loaded[u], 16)
                    sp.dma_start(dsts[u][:, PT:TILES], dst_parts[1][chunk]).then_inc(s_dst_loaded[u], 16)
                else:
                    sp.dma_start(dsts[u][:, :], dst_whole[chunk]).then_inc(s_dst_loaded[u], 16)

            def load_edges(chunk, u, picked=False):
                if picked:
                    sp.dma_start(edges[u][:, 0:PT * D], edge_parts[0][chunk]).then_inc(s_edges_loaded[u], 16)
                    sp.dma_start(edges[u][:, PT * D:TILES * D],
                                 edge_parts[1][chunk]).then_inc(s_edges_loaded[u], 16)
                else:
                    sp.dma_start(edges[u][:, :], edge_whole[chunk]).then_inc(s_edges_loaded[u], 16)

            def load_round_src(r):
                sp.dma_start(src_all[:, :, :], src_rounds[r].unsqueeze(0)
                             .to_broadcast([P, SLOTS, P])).then_inc(s_round_src, 16)

            for u in range(2):
                load_src(u, u)
            sp.dma_start(m_stage[:, :, :, :], M_W.rearrange("o (h d) -> o h d", h=2).unsqueeze(2)
                         .to_broadcast([D, 2, 2, D])).then_inc(s_w_loaded, 16)
            sp.dma_start(u_stage[:, :], U_W).then_inc(s_w_loaded, 16)
            sp.dma_start(m_bias[:, 0, :], M_b.rearrange("(a d) -> a d", a=1)
                         .to_broadcast([P, D])).then_inc(s_bias_loaded, 16)
            sp.dma_start(u_bias[:, :], U_b.rearrange("(d a) -> d a", a=1)).then_inc(s_bias_loaded, 16)
            load_src(2, 2)
            for u in range(SLOTS):
                load_edges(u, u)
                load_dst(u, u)
            load_round_src(FIRST_PICKED)
            sp.wait_ge(s_last_cleared, 1)
            for tail, last, loaded in ((tail_parts(src), src_last, s_src_last_loaded),
                                       (tail_parts(dst), dst_last, s_dst_last_loaded)):
                sp.dma_start(last[:, 0:TW], tail[0]).then_inc(loaded, 16)
                sp.dma_start(last[0:TP, TW:TT], tail[1]).then_inc(loaded, 16)

            def load_next_src(r, u):
                sp.wait_ge(s_gathered[u], gathered_by(r - 1))
                load_src(r * SLOTS + u, u, not (isinstance(r, int) and r < FIRST_PICKED))

            for g, (b0, b1) in enumerate(groups):
                sp.wait_ge(s_Y, g + 1)
                full = min(b1, NFULL)
                if full > b0:
                    sp.dma_start(Y_blocks[:, b0:full, :], Y[:, b0:full, :]).then_inc(s_Y_stored, 16)
                if b1 > NFULL:
                    sp.dma_start(Y_rows[NFULL * W:N, :], Y[0:NLAST, NFULL, :]).then_inc(s_Y_stored, 16)
                if g == len(groups) // 2:
                    load_next_src(1, 0)

            def load_chunk(r, u):
                chunk = r * SLOTS + u
                picked = not (isinstance(r, int) and r < FIRST_PICKED)
                if picked:
                    load_next_src(r, u)
                sp.wait_ge(s_edges_T, chunk - (SLOTS - 1))
                load_edges(chunk, u, picked)
                sp.wait_ge(s_chunk_added, chunk - (SLOTS - 1))
                load_dst(chunk, u, picked)

            for u in range(1, SLOTS):
                load_next_src(1, u)
            for u in range(SLOTS):
                load_chunk(1, u)
            with sp.Fori(2, ROUNDS - 1) as r:
                load_chunk(r, 0)
                sp.wait_ge(s_prep, r * 4 - 4)
                load_round_src(r + 1)
                for u in range(1, SLOTS):
                    load_chunk(r, u)
            for u in range(SLOTS):
                load_chunk(ROUNDS - 1, u)
            sp.wait_ge(s_edges_T, NC - (SLOTS - 1))
            sp.dma_start(edges[0][:, 0:TW * D], edge_tail[0]).then_inc(s_edges_loaded[0], 16)
            sp.dma_start(edges[0][0:TP, TW * D:TT * D], edge_tail[1]).then_inc(s_edges_loaded[0], 16)

            for g, (b0, b1) in enumerate(groups):
                sp.wait_ge(s_normed, g + 1)
                full = min(b1, NFULL)
                if full > b0:
                    sp.dma_start(out_blocks[:, b0:full, :], h[:, b0:full, :]).then_inc(s_out, 16)
                if b1 > NFULL:
                    sp.dma_start(out[NFULL * W:N, :], h[0:NLAST, NFULL, :]).then_inc(s_out, 16)
            sp.wait_ge(s_out, 16 * stores)

        @block.gpsimd
        def _(pool):
            nc.gpsimd.memset(ident[:, :], 0.0).then_inc(s_ident, 1)
            pool.wait_ge(s_ident, 1)
            nc.gpsimd.affine_select(out=ident[:, :], in_=ident[:, :], compare_op=ALU.not_equal, fill=1.0,
                                    base=0, pattern=[[-1, P]], channel_multiplier=1).then_inc(s_ident, 1)
            nc.gpsimd.iota(count[:, :], pattern=[[1, W]], base=0, channel_multiplier=0)
            nc.gpsimd.iota(window_start_i[:, :], pattern=[[W, NW]], base=0,
                           channel_multiplier=0)
            nc.gpsimd.iota(node_i[:, :], pattern=[[1, 1]], base=0, channel_multiplier=1).then_inc(s_iota, 1)

            def gather(u, index, tiles=TILES, last_parts=P, rows=gathered, table=Y_rows):
                for j in range(tiles):
                    parts = last_parts if j == tiles - 1 else P
                    nc.gpsimd.indirect_dma_start(
                        out=rows[u][0:parts, j * D:(j + 1) * D], out_offset=None, in_=table,
                        in_offset=bass.IndirectOffsetOnAxis(ap=index[0:parts, j:j + 1], axis=0),
                    ).then_inc(s_gathered[u], 16)

            for u in range(SLOTS):
                pool.wait_ge(s_src_loaded[u], 16)
                gather(u, srcs[u], rows=x_rows, table=x[:, :])
            pool.wait_ge(s_Y_stored, 16 * stores)
            for u in range(SLOTS):
                pool.wait_ge(s_src_loaded[u], 2 * 16)
                gather(u, srcs[u])
            with pool.Fori(FIRST_PICKED, ROUNDS) as r:
                for u in range(SLOTS):
                    pool.wait_ge(s_src_loaded[u], (r + 1) * 16)
                    pool.wait_ge(s_rows_added, r * SLOTS + (u - SLOTS + 1))
                    pool.sem_inc(s_slot_taken, 1)
                    gather(u, srcs[u], PT)
            pool.wait_ge(s_src_last_loaded, 2 * 16)
            pool.wait_ge(s_rows_added, NC - SLOTS + 1)
            gather(0, src_last, TT, TP)

            def apply_to_rows(g, values, op, done):
                b0, b1 = groups[g]
                nc.gpsimd.tensor_tensor(h[:, b0:b1, :], h[:, b0:b1, :],
                                        values[:, b0:b1].unsqueeze(2).to_broadcast([P, b1 - b0, D]),
                                        op).then_inc(done, 1)

            for g in range(len(groups) + LAG + 1):
                if g < len(groups):
                    pool.wait_ge(s_mean, g + 1)
                    apply_to_rows(g, mean, ALU.add, s_centered)
                if g > LAG:
                    pool.wait_ge(s_scale, g - LAG)
                    apply_to_rows(g - LAG - 1, std, ALU.mult, s_normed)

        @block.scalar
        def _(act):
            act.dma_start(xb[:, 0:FB, :], x_blocks[:, 0:FB, :]).then_inc(s_x_loaded, 16)
            act.dma_start(xb[:, FB:X_FIRST, :], x_blocks[:, FB:X_FIRST, :]).then_inc(s_x_more_loaded, 16)
            act.dma_start(dst_check[0], dst_rows[0:P, :]).then_inc(s_check_loaded, 16)
            act.dma_start(dst_check[1][0:NB, :], dst_rows[P:NC, :]).then_inc(s_check_more_loaded, 16)
            act.dma_start(dst_check_last[:, :], dst_tail_row).then_inc(s_check_more_loaded, 16)
            act.dma_start(xb[:, X_FIRST:NFULL, :], x_blocks[:, X_FIRST:NFULL, :]).then_inc(s_x_rest_loaded, 16)
            act.wait_ge(s_cleared, 1)
            act.dma_start(xb[0:NLAST, NFULL, :], x[NFULL * W:N, :]).then_inc(s_x_rest_loaded, 16)

            def copy_block_start(b0, b1):
                nc.scalar.copy(block_start[:, b0:b1, :], window_start_i[:, b0:b1].unsqueeze(2)
                               .to_broadcast([P, b1 - b0, P])).then_inc(s_block_start, 1)

            act.wait_ge(s_eps, 1)
            nc.scalar.activation(std[:, 0:1], eps_col[:, 0:1], ACT.Sqrt)
            act.wait_ge(s_iota, 1)
            copy_block_start(0, FB)

            def copy_part(target, source):
                nc.scalar.copy(target, source).then_inc(s_Y_split, 1)

            def copy_first(g):
                b0, b1 = groups[g]
                act.wait_ge(s_Y, g + 1)
                copy_part(Y_hm[:, b0:b1, 0:D], Y[:, b0:b1, :])

            for g, (b0, b1) in enumerate(groups):
                act.wait_ge(s_x_T, g + 1)
                pairs, rows = -(-(b1 - b0) // 2), min(b1 - b0, 2) * D
                nc.scalar.copy(x_pairs_T[0:rows, b0 // 2 * W:(b0 // 2 + pairs) * W],
                               p_messages[g % SLOTS][0:rows, 0:pairs * W]).then_inc(s_x_copied, 1)
                if g >= 2:
                    copy_first(g - 2)
            for g in range(len(groups) - 2, len(groups)):
                copy_first(g)
            copy_block_start(FB, NW)

            def copy_edges_T(chunk, u, pairs=PAIRS):
                act.wait_ge(s_edges_T, chunk + 1)
                nc.scalar.copy(edges_T[u][:, 0:pairs * P], p_edges_T[:, 0:pairs * P]).then_inc(s_edges_T_copied, 1)

            def rectify(chunk, u, pairs=PAIRS):
                act.wait_ge(s_rows_added, chunk + 1)
                nc.scalar.activation(messages[u][:, 0:pairs * P], p_messages[u][:, 0:pairs * P],
                                     ACT.Relu).then_inc(s_messages, 1)

            copy_edges_T(0, 0)

            def chunk_steps(r, u):
                chunk = r * SLOTS + u
                copy_edges_T(chunk + 1, (u + 1) % SLOTS)
                rectify(chunk, u)

            h0, h1 = slice(0, X_FIRST), slice(X_FIRST, NW)
            parts = [(X_FIRST // FB, Y_hm[:, h0, D:2 * D], sq[:, h0, :]),
                     (len(groups), Y_hm[:, h1, D:2 * D], sq[:, h1, :]),
                     (len(groups) + 1, Y_l[:, h0, :], sq[:, h0, :]),
                     (len(groups) + 2, Y_l[:, h1, :], sq[:, h1, :])]

            def copy_x_rows_T(u):
                act.wait_ge(s_x_rows_T, u + 1)
                nc.scalar.copy(x_rows_T[:, :], p_x_rows_T[:, 0:PAIRS * P]).then_inc(s_x_rows_T_copied, 1)

            copy_x_rows_T(0)
            for u in range(SLOTS):
                copy_edges_T(u + 1, (u + 1) % SLOTS)
                if u < SLOTS - 1:
                    copy_x_rows_T(u + 1)
                rectify(u, u)
                for rest, part, source in parts[u:u + 1] + (parts[SLOTS:] if u == SLOTS - 1 else []):
                    act.wait_ge(s_Y_rest, rest)
                    copy_part(part, source)
            with act.Fori(1, ROUNDS - 1) as r:
                for u in range(SLOTS):
                    chunk_steps(r, u)
                act.wait_ge(s_picked, r)
                nc.scalar.copy(picked_hm[:, :], p_picked_hm[:, 0:SLOTS * P])
                nc.scalar.copy(picked_l[:, :], p_picked_l[:, 0:SLOTS * P]).then_inc(s_picked_copied, 1)
            x_rows_of = XZ[0:D, 0:NFULL * W].rearrange("d (q two w) -> d q two w", two=2, w=W)
            pairs_T = x_pairs_T[:, 0:NFULL // 2 * W].rearrange("p (q w) -> p q w", w=W)
            for u in range(SLOTS):
                chunk_steps(ROUNDS - 1, u)
                if u < 2:
                    nc.scalar.copy(x_rows_of[:, :, u, :], pairs_T[u * D:(u + 1) * D, :, :])
            nc.scalar.copy(XZ[0:D, NFULL * W:NW * W],
                           x_pairs_T[0:D, NFULL // 2 * W:(NFULL // 2 + 1) * W]).then_inc(s_XZ, 1)
            rectify(NC, 0, TQ)

            act.wait_ge(s_bias_loaded, 2 * 16)

            def relu_update(k):
                b0, b1 = x_groups[k]
                if k >= SLOTS:
                    act.wait_ge(s_update, k - SLOTS + 1)
                act.wait_ge(s_update_T, k + 1)
                nc.scalar.activation(update_T[k % SLOTS][:, 0:(b1 - b0) * W],
                                     p_update_T[k % SLOTS][0:D, 0:(b1 - b0) * W],
                                     ACT.Relu, bias=u_bias[:, 0:1]).then_inc(s_update_relu, 1)

            def square(g):
                b0, b1 = groups[g]
                act.wait_ge(s_centered, g + 1)
                nc.scalar.activation(sq[:, b0:b1, :], h[:, b0:b1, :], ACT.Square).then_inc(s_squared, 1)

            def root(g):
                b0, b1 = groups[g]
                act.wait_ge(s_var, g + 1)
                nc.scalar.activation(std[:, b0:b1], var[:, b0:b1], ACT.Sqrt, bias=eps_col[:, 0:1],
                                     scale=1.0 / D).then_inc(s_std, 1)

            for g in range(len(groups) + LAG + 1):
                for k in range(g * FB // XB, min((g + 1) * FB // XB, len(x_groups))):
                    relu_update(k)
                if LAG <= g < len(groups) + LAG:
                    square(g - LAG)
                if g > LAG:
                    root(g - LAG - 1)

        @block.vector
        def _(dve):
            chain = [0]

            def link(ins):
                chain[0] += 1
                ins.then_inc(s_dve, 1)
                dve.wait_ge(s_dve, chain[0])

            nc.vector.memset(xb[:, NFULL, :], 0.0).then_inc(s_cleared, 1)
            nc.vector.memset(eps_col[:, :], EPS).then_inc(s_eps, 1)
            nc.vector.memset(dst_last[:, :], -1).then_inc(s_last_cleared, 1)
            nc.vector.memset(ones[:, :], 1.0)
            nc.vector.memset(w_gathered[:, :], 0.0)
            link(nc.vector.memset(w_edges[:, :], 0.0))
            nc.vector.memset(XZ[D:P, 0:X_FIRST * W], 0.0)
            dve.wait_ge(s_iota, 1)
            nc.vector.tensor_copy(p_count, count[:, :])
            nc.vector.tensor_copy(node[:, :], node_i[:, :])
            nc.vector.tensor_copy(window_start[:, :], window_start_i[:, :])
            dve.wait_ge(s_w_T, 1)
            nc.vector.tensor_copy(w_gathered[0:D, 0:D], p_setup[0:D, 0:D])
            nc.vector.tensor_copy(w_gathered[D:P, D:2 * D], p_setup[D:P, 0:D])
            nc.vector.tensor_copy(w_edges[0:D, 0:D], p_setup[0:D, D:2 * D])
            nc.vector.tensor_copy(w_edges[D:P, D:2 * D], p_setup[D:P, D:2 * D])
            nc.vector.tensor_copy(w_update[:, :], p_setup[:, 2 * D:3 * D]).then_inc(s_w_ready, 1)
            for half in range(2):
                nc.vector.tensor_copy(ident_stack[half * D:(half + 1) * D, :],
                                      ident[half * D:(half + 1) * D, half * D:(half + 1) * D])

            def check_dst(k, n, rows):
                nc.vector.tensor_reduce(least[0:n, k:k + 1], rows, AX.X, ALU.min)
                link(nc.vector.tensor_reduce(most[0:n, k:k + 1], rows, AX.X, ALU.max))
                return nc.vector.tensor_tensor(span[0:n, k:k + 1], most[0:n, k:k + 1], least[0:n, k:k + 1],
                                               ALU.subtract)

            def first_rest(g):
                b0, b1 = groups[g]
                dve.wait_ge(s_Y_split, g + 1)
                nc.vector.tensor_tensor(sq[:, b0:b1, :], Y[:, b0:b1, :], Y_hm[:, b0:b1, 0:D],
                                        ALU.subtract).then_inc(s_Y_rest, 1)

            def second_rest(half, part):
                dve.wait_ge(s_Y_split, part)
                nc.vector.tensor_tensor(sq[:, half, :], sq[:, half, :], Y_hm[:, half, D:2 * D],
                                        ALU.subtract).then_inc(s_Y_rest, 1)

            dve.wait_ge(s_check_loaded, 16)
            check_dst(0, P, dst_check[0])
            dve.wait_ge(s_check_more_loaded, 2 * 16)
            check_dst(1, NB, dst_check[1][0:NB, :])
            check_dst(2, 1, dst_check_last[:, :]).then_inc(s_least, 1)
            dve.wait_ge(s_bias_loaded, 2 * 16)
            for g, (b0, b1) in enumerate(groups):
                dve.wait_ge(s_Y_summed, g + 1)
                nc.vector.tensor_tensor(Y[:, b0:b1, :],
                                        p_Y[g % 2][:, 0:(b1 - b0) * D].rearrange("p (b d) -> p b d", d=D),
                                        m_bias[:, :, :].to_broadcast([P, b1 - b0, D]), ALU.add).then_inc(s_Y, 1)
                if g >= 2:
                    first_rest(g - 2)
            dve.wait_ge(s_least_T, 1)
            nc.vector.tensor_copy(base_row[:, 0:NC], p_setup[0:1, 0:NC])
            nc.vector.tensor_copy(base_row[:, NC:NC + 1], least[0:1, 2:3]).then_inc(s_base_row, 1)
            nc.vector.tensor_copy(base_i[:, 0:NC], p_setup[0:1, 0:NC])
            nc.vector.tensor_copy(base_i[:, NC:NC + 1], least[0:1, 2:3])
            link(nc.vector.reduce_max(widest[:, :], p_setup[0:1, 2 * P:2 * P + NC], AX.X))
            link(nc.vector.tensor_tensor(widest[:, :], widest[:, :], span[0:1, 2:3], ALU.max))
            nc.vector.tensor_scalar(spread[:, :], widest[:, :], float(W), None, ALU.is_ge).then_inc(s_base, 1)
            dve.wait_ge(s_base_spread, 1)
            nc.vector.tensor_copy(base[:, 0:NC + 1], p_base[:, 0:NC + 1]).then_inc(s_base_copied, 1)
            dve.wait_ge(s_base_copied, 1)
            dve.wait_ge(s_base, 1)
            for g in range(len(groups) - 2, len(groups)):
                first_rest(g)
            nc.vector.memset(XZ[D:P, X_FIRST * W:], 0.0)
            dve.wait_ge(s_block_start, 2)

            count_b = p_count.unsqueeze(1).to_broadcast([P, TILES, W])

            def compare(u, start, nodes, tiles):
                nc.vector.scalar_tensor_tensor(
                    out=onehot[u][:, 0:tiles, :], in0=count_b[:, 0:tiles, :], scalar=start,
                    in1=nodes[:, :].unsqueeze(2).to_broadcast([P, tiles, W]),
                    op0=ALU.add, op1=ALU.is_equal).then_inc(s_onehot, 1)

            def match_src(r):
                dve.wait_ge(s_round_src, r * 16)
                nc.vector.tensor_scalar(src_low[:, :, :], src_all[:, :, :], P - 1, None,
                                        ALU.bitwise_and).then_inc(s_prep, 1)
                dve.wait_ge(s_prep, r * 4 - 3)
                nc.vector.scalar_tensor_tensor(out=src_start[:, :, :], in0=src_low[:, :, :], scalar=-1.0,
                                               in1=src_all[:, :, :], op0=ALU.mult, op1=ALU.add)
                nc.vector.tensor_scalar(src_miss[:, :, :], src_low[:, :, :], node[:, 0:1], MISS,
                                        ALU.not_equal, ALU.mult).then_inc(s_prep, 1)
                dve.wait_ge(s_prep, r * 4 - 2)
                nc.vector.tensor_tensor(src_start[:, :, :], src_start[:, :, :], src_miss[:, :, :],
                                        ALU.add).then_inc(s_prep, 1)
                dve.wait_ge(s_prep, r * 4 - 1)
                nc.vector.tensor_scalar(src_match, src_start[:, :, :].rearrange("p u e -> p (u e)").bitcast(i32),
                                        0, None, ALU.bitwise_or).then_inc(s_prep, 1)
                dve.wait_ge(s_prep, r * 4)

            def compare_src(k):
                b0, b1 = PARTS[k]
                for u in range(SLOTS):
                    match = src_match.bitcast(bf16)[:, u * P:(u + 1) * P]
                    last = nc.vector.tensor_tensor(onehot_src[k][:, :, u, :],
                                                   match.unsqueeze(1).to_broadcast([P, b1 - b0, P]),
                                                   block_start[:, b0:b1, :], ALU.is_equal)
                last.then_inc(s_onehot_src, 1)

            def pick(r, u):
                if u == 0:
                    match_src(r)
                compare_src(u)

            def add_m_bias(chunk, u):
                dve.wait_ge(s_summed, chunk + 1)
                sums = p_messages[u][:, :].rearrange("p (t d) -> p t d", d=D)
                nc.vector.tensor_tensor(sums, sums, m_bias[:, :, :].to_broadcast([P, TILES, D]),
                                        ALU.add).then_inc(s_rows_added, 1)

            def add_rows(chunk, u, gathered_count, tiles):
                dve.wait_ge(s_summed, chunk + 1)
                dve.wait_ge(s_gathered[u], gathered_count)
                sums = p_messages[u][:, 0:tiles * D]
                nc.vector.tensor_tensor(sums, sums, gathered[u][:, 0:tiles * D],
                                        ALU.add).then_inc(s_rows_added, 1)

            def one_window(chunk, u, nodes, loaded, loaded_count, tiles=TILES, following=None):
                start = dve.value_load(base_i[0:1, bass.ds(chunk, 1)], min_val=0, max_val=N - 1)
                dve.wait_ge(s_window, chunk + 1)
                columns = XZ[D:P, bass.ds(start, W)]
                nc.vector.tensor_tensor(columns, columns, p_windows[u],
                                        ALU.add).then_inc(s_chunk_added, 1)
                if following is not None:
                    compare_ahead(chunk + 1, *following)

            def compare_ahead(chunk, u, nodes, loaded, loaded_count, tiles=TILES):
                dve.wait_ge(loaded, loaded_count)
                compare(u, base[:, bass.ds(chunk, 1)], nodes, tiles)

            def all_windows(chunk, u, nodes, loaded, loaded_count, tiles=TILES, following=None):
                with dve.Fori(0, NW) as w:
                    dve.wait_ge(loaded, loaded_count)
                    compare(u, window_start[:, bass.ds(w, 1)], nodes, tiles)
                    dve.wait_ge(s_window, chunk * NW + w + 1)
                    columns = XZ[D:P, bass.ds(w * W, W)]
                    nc.vector.tensor_tensor(columns, columns, p_windows[u],
                                            ALU.add).then_inc(s_window_added, 1)
                dve.wait_ge(s_window_added, (chunk + 1) * NW)
                dve.sem_inc(s_chunk_added, 1)

            def chunks(windows):
                last_chunk = (0, dst_last, s_dst_last_loaded, 2 * 16, TT)

                def nodes_of(r, u):
                    return (u, dsts[u], s_dst_loaded[u], loaded_by(r))

                def following(r, u):
                    return nodes_of(r + (u == SLOTS - 1), (u + 1) % SLOTS)

                def round_steps(r, tiles, more=True):
                    for u in range(SLOTS):
                        add_rows(r * SLOTS + u, u, gathered_by(r), tiles)
                        if u < SLOTS - 1:
                            pick(r, u + 1)
                        elif more:
                            pick(r + 1, 0)
                        windows(r * SLOTS + u, *nodes_of(r, u), following=following(r, u))

                if windows is one_window:
                    compare_ahead(0, *nodes_of(0, 0))
                for u in range(SLOTS):
                    add_m_bias(u, u)
                    if u == SLOTS - 1:
                        pick(1, 0)
                    windows(u, *nodes_of(0, u), following=following(0, u))
                    if u < 2:
                        second_rest((slice(0, X_FIRST), slice(X_FIRST, NW))[u], len(groups) + 1 + u)
                round_steps(1, TILES)
                with dve.Fori(FIRST_PICKED, ROUNDS - 2) as r:
                    round_steps(r, PT)
                round_steps(ROUNDS - 2, PT, more=False)
                for u in range(SLOTS):
                    add_rows(NC - SLOTS + u, u, gathered_by(ROUNDS - 1), PT)
                    windows(NC - SLOTS + u, *nodes_of(ROUNDS - 1, u),
                            following=last_chunk if u == SLOTS - 1 else following(ROUNDS - 1, u))
                add_rows(NC, 0, gathered_by(ROUNDS - 1) + TT * 16, TT)
                windows(NC, *last_chunk)

            is_spread = dve.value_load(spread[0:1, 0:1], min_val=0, max_val=1)
            with dve.If(is_spread == 0):
                chunks(one_window)
            with dve.Else():
                chunks(all_windows)

            def add_x(g):
                b0, b1 = groups[g]
                hg = h[:, b0:b1, :]
                dve.wait_ge(s_update, min((g + 1) * FB // XB, len(x_groups)))
                nc.vector.tensor_tensor(hg, p_update[g % 2][:, 0:(b1 - b0) * D].rearrange("p (b d) -> p b d", d=D),
                                        xb[:, b0:b1, :], ALU.add).then_inc(s_h, 1)
                dve.wait_ge(s_h, g + 1)
                link(nc.vector.reduce_sum(total[:, b0:b1], hg, AX.X))
                nc.vector.tensor_scalar(mean[:, b0:b1], total[:, b0:b1], -1.0 / D, None,
                                        ALU.mult).then_inc(s_mean, 1)

            def sum_squares(g):
                b0, b1 = groups[g]
                dve.wait_ge(s_squared, g + 1)
                nc.vector.reduce_sum(var[:, b0:b1], sq[:, b0:b1, :], AX.X).then_inc(s_var, 1)

            def invert(g):
                b0, b1 = groups[g]
                dve.wait_ge(s_std, g + 1)
                nc.vector.reciprocal(std[:, b0:b1], std[:, b0:b1]).then_inc(s_scale, 1)

            for g in range(len(groups) + LAG + 1):
                if g < len(groups):
                    add_x(g)
                if LAG <= g < len(groups) + LAG:
                    sum_squares(g - LAG)
                if g > LAG:
                    invert(g - LAG - 1)

        @block.tensor
        def _(pe):
            def spread_base():
                pe.wait_ge(s_least, 1)
                for k, n in ((0, P), (1, NB)):
                    nc.tensor.transpose(p_setup[0:1, k * P:k * P + n], least[0:n, k:k + 1], ident[0:n, 0:n])
                    last = nc.tensor.transpose(p_setup[0:1, (2 + k) * P:(2 + k) * P + n], span[0:n, k:k + 1],
                                               ident[0:n, 0:n])
                last.then_inc(s_least_T, 1)
                pe.wait_ge(s_base_row, 1)
                nc.tensor.matmul(p_base[:, 0:NC + 1], ones[0:1, :], base_row[0:1, 0:NC + 1],
                                 start=True, stop=True).then_inc(s_base_spread, 1)

            def transpose_x(g):
                if g < 2:
                    pe.wait_ge((s_x_loaded, s_x_more_loaded)[g], 16)
                if groups[g][0] == X_FIRST:
                    pe.wait_ge(s_x_rest_loaded, 2 * 16)
                if g >= SLOTS:
                    pe.wait_ge(s_x_copied, g - SLOTS + 1)
                b0, b1 = groups[g]
                for b in range(b0, b1, 2):
                    n = min(2, b1 - b)
                    last = nc.tensor.transpose(p_messages[g % SLOTS][0:n * D, (b - b0) // 2 * W:((b - b0) // 2 + 1) * W],
                                               xb[:, b:b + n, :].rearrange("p n d -> p (n d)"), ident[:, :])
                last.then_inc(s_x_T, 1)

            def sum_Y(g):
                b0, b1 = groups[g]
                pe.wait_ge(s_x_copied, g + 1)
                if g >= 2:
                    pe.wait_ge(s_Y, g - 1)
                for b in range(b0, b1, 2):
                    width = min(2, b1 - b) * D
                    last = nc.tensor.matmul(p_Y[g % 2][:, (b - b0) * D:(b - b0) * D + width],
                                            x_pairs_T[0:width, b // 2 * W:(b // 2 + 1) * W],
                                            w_gathered[0:width, 0:width], start=True, stop=True)
                last.then_inc(s_Y_summed, 1)

            pe.wait_ge(s_ident, 2)
            pe.wait_ge(s_w_loaded, 2 * 16)
            for k, w in enumerate((m_stage[:, 0, :, :].rearrange("o t d -> o (t d)"),
                                   m_stage[:, 1, :, :].rearrange("o t d -> o (t d)"), u_stage[:, :])):
                last = nc.tensor.transpose(p_setup[:, k * D:(k + 1) * D], w, ident[0:D, 0:D])
            last.then_inc(s_w_T, 1)
            transpose_x(0)
            pe.wait_ge(s_w_ready, 1)
            for g in range(1, len(groups)):
                transpose_x(g)
                sum_Y(g - 1)
            sum_Y(len(groups) - 1)
            pe.wait_ge(s_Y, len(groups))
            spread_base()

            def transpose_edges(u, edges_count, pairs=PAIRS):
                pe.wait_ge(s_edges_loaded[u], edges_count)
                for q in range(pairs):
                    last = nc.tensor.transpose(p_edges_T[:, q * P:(q + 1) * P], edges[u][:, q * P:(q + 1) * P],
                                               ident[:, :])
                last.then_inc(s_edges_T, 1)

            def add_edges(chunk, u, pairs=PAIRS, done=False):
                pe.wait_ge(s_edges_T_copied, chunk + 1)
                for q in range(pairs):
                    last = nc.tensor.matmul(p_messages[u][:, q * P:(q + 1) * P], edges_T[u][:, q * P:(q + 1) * P],
                                            w_edges[:, :], start=(q == 0), stop=(done and q == pairs - 1))
                if done:
                    last.then_inc(s_summed, 1)

            def add_picked(u):
                nc.tensor.matmul(p_messages[u][:, PT * D:TILES * D], picked_hm[:, u * P:(u + 1) * P],
                                 ident_stack[:, :], start=False, stop=False)
                nc.tensor.matmul(p_messages[u][:, PT * D:TILES * D], picked_l[:, u * P:(u + 1) * P],
                                 ident_stack[:, :], start=False, stop=True).then_inc(s_summed, 1)

            def transpose_x_rows(u):
                pe.wait_ge(s_gathered[u], gathered_by(0))
                for q in range(PAIRS):
                    last = nc.tensor.transpose(p_x_rows_T[:, q * P:(q + 1) * P], x_rows[u][:, q * P:(q + 1) * P],
                                               ident[:, :])
                last.then_inc(s_x_rows_T, 1)

            def add_x_rows(u):
                pe.wait_ge(s_x_rows_T_copied, u + 1)
                for q in range(PAIRS):
                    last = nc.tensor.matmul(p_messages[u][:, q * P:(q + 1) * P], x_rows_T[:, q * P:(q + 1) * P],
                                            w_gathered[:, :], start=False, stop=(q == PAIRS - 1))
                last.then_inc(s_summed, 1)

            def pick(chunk, k):
                pe.wait_ge(s_onehot_src, chunk - (SLOTS - 1))
                b0, b1 = PARTS[k]

                def edges_of(b):
                    return onehot_src[k][:, b - b0, :, :].rearrange("p u e -> p (u e)")

                for b in range(b0, b1, 2):
                    pair = range(b, min(b + 2, b1))
                    for c in pair:
                        nc.tensor.matmul(p_picked_hm[:, 0:SLOTS * P], Y_hm[:, c, :], edges_of(c),
                                         start=(c == 0), stop=(c == NW - 1))
                    for c in pair:
                        half = (c - b) * D
                        last = nc.tensor.matmul(p_picked_l[half:half + D, 0:SLOTS * P], Y_l[:, c, :], edges_of(c),
                                                start=(c < 2), stop=(c >= NW - 2))
                if k == len(PARTS) - 1:
                    last.then_inc(s_picked, 1)

            def sum_window(u, tiles):
                for j in range(tiles):
                    last = nc.tensor.matmul(p_windows[u], messages[u][:, j * D:(j + 1) * D],
                                            onehot[u][:, j, :], start=(j == 0), stop=(j == tiles - 1))
                last.then_inc(s_window, 1)

            def one_window(chunk, u, tiles=TILES):
                pe.wait_ge(s_messages, chunk + 1)
                pe.wait_ge(s_onehot, chunk + 1)
                sum_window(u, tiles)

            def all_windows(chunk, u, tiles=TILES):
                with pe.Fori(0, NW) as w:
                    pe.wait_ge(s_messages, chunk + 1)
                    pe.wait_ge(s_onehot, chunk * NW + w + 1)
                    sum_window(u, tiles)

            def chunks(windows):
                transpose_edges(0, loaded_by(0))
                pe.wait_ge(s_base_copied, 1)
                transpose_x_rows(0)
                add_edges(0, 0)
                add_x_rows(0)
                for u in range(SLOTS):
                    v = (u + 1) % SLOTS
                    transpose_edges(v, loaded_by(int(v == 0)))
                    if v > 0:
                        transpose_x_rows(v)
                    add_edges(u + 1, v, done=(v == 0))
                    if v > 0:
                        add_x_rows(v)
                    windows(u, u)
                pe.wait_ge(s_Y_split, len(groups) + 4)
                for u in range(SLOTS):
                    chunk, v = SLOTS + u, (u + 1) % SLOTS
                    transpose_edges(v, loaded_by(1 + (v == 0)))
                    pick(chunk, u)
                    windows(chunk, u)
                    add_edges(chunk + 1, v, done=(v > 0))
                with pe.Fori(FIRST_PICKED, ROUNDS - 1) as r:
                    for u in range(SLOTS):
                        chunk, v = r * SLOTS + u, (u + 1) % SLOTS
                        transpose_edges(v, loaded_by(r + (v == 0)))
                        if u == 0:
                            pe.wait_ge(s_picked_copied, r - 1)
                        add_picked(u)
                        pick(chunk, u)
                        windows(chunk, u)
                        add_edges(chunk + 1, v)
                for u in range(SLOTS):
                    chunk, v = (ROUNDS - 1) * SLOTS + u, (u + 1) % SLOTS
                    last = u == SLOTS - 1
                    transpose_edges(v, loaded_by(ROUNDS - 1) + (32 if last else 0), TQ if last else PAIRS)
                    if u == 0:
                        pe.wait_ge(s_picked_copied, ROUNDS - 2)
                    add_picked(u)
                    windows(chunk, u)
                    add_edges(chunk + 1, v, TQ if last else PAIRS, done=last)
                windows(NC, 0, TT)

            pe.wait_ge(s_base, 1)
            is_spread = pe.value_load(spread[0:1, 0:1], min_val=0, max_val=1)
            with pe.If(is_spread == 0):
                chunks(one_window)
            with pe.Else():
                chunks(all_windows)

            pe.wait_ge(s_chunk_added, NC + 1)
            pe.wait_ge(s_XZ, 1)

            def sum_update(k):
                b0, b1 = x_groups[k]
                if k >= SLOTS:
                    pe.wait_ge(s_update_relu, k - SLOTS + 1)
                nc.tensor.matmul(p_update_T[k % SLOTS][0:D, 0:(b1 - b0) * W], w_update[:, :],
                                 XZ[:, b0 * W:b1 * W], start=True, stop=True).then_inc(s_update_T, 1)

            def turn_update(k):
                g = k * XB // FB
                first = groups[g][0]
                if g >= 2:
                    pe.wait_ge(s_h, g - 1)
                pe.wait_ge(s_update_relu, k + 1)
                b0, b1 = x_groups[k]
                for b in range(b0, b1):
                    last = nc.tensor.transpose(p_update[g % 2][:, (b - first) * D:(b - first + 1) * D],
                                               update_T[k % SLOTS][:, (b - b0) * W:(b - b0 + 1) * W],
                                               ident[0:D, 0:D])
                last.then_inc(s_update, 1)

            for k in range(len(x_groups) + 1):
                if k < len(x_groups):
                    sum_update(k)
                if k >= 1:
                    turn_update(k - 1)


_INS = ['x', 'src', 'dst', 'edge_attr_64', 'L0_gnn_M_W', 'L0_gnn_M_b', 'L0_gnn_U_W', 'L0_gnn_U_b']
_OUTS = [((6250, 64), 'float32')]


def kernel(**inputs):
    import numpy as _np
    import concourse.bacc as _bacc
    from concourse import mybir as _mybir
    from concourse.bass_utils import run_bass_kernel_spmd as _run

    nc = _bacc.Bacc("TRN2", target_bir_lowering=False, num_devices=1)
    arrays, args = {}, []
    for name in _INS:
        a = _np.ascontiguousarray(inputs[name])
        arrays[f"in_{name}_dram"] = a
        args.append(nc.dram_tensor(f"in_{name}_dram", a.shape, _mybir.dt.from_np(a.dtype), kind="ExternalInput").ap())
    for i, (shape, dtype) in enumerate(_OUTS):
        dt = _mybir.dt.from_np(_np.dtype(dtype))
        args.append(nc.dram_tensor(f"out_{i}_dram", shape, dt, kind="ExternalOutput").ap())
    gnn_residual_layernorm_kernel(nc, *args)
    r = _run(nc, [arrays], core_ids=[0])
    return r.results[0]["out_0_dram"]
```
